# Optimizing a Trainium2 kernel written in Bass

```python
import numpy as np
import jax
import jax.numpy as jnp

def _softmax(x, axis=-1):
    return jax.nn.softmax(x, axis=axis)

def _gelu(x):
    return jax.nn.gelu(x, approximate=True)

def _silu(x):
    return jax.nn.silu(x)

def _sigmoid(x):
    return jax.nn.sigmoid(x)

def _layernorm(x, axis=-1, eps=1e-05):
    m = jnp.mean(x, axis=axis, keepdims=True)
    v = jnp.var(x, axis=axis, keepdims=True)
    return (x - m) / jnp.sqrt(v + eps)

def _scatter_add(tgt, idx, src, axis=0):
    return tgt.at[idx].add(src)

def _segment_sum(src, seg, n):
    return jax.ops.segment_sum(src, seg, n)
kernel_name = 'mk_adaln_d1_jaxref_r8_9bf67d'

def setup_inputs(seed: int=0):
    np.random.seed(seed)
    _w = jnp.asarray

    def _L0_attn_setup():
        import jax, jax.numpy as jnp
        import numpy as np
        DMODEL = 256
        HEADS = 16
        DHEAD = DMODEL // HEADS
        key = jax.random.key(seed)
        ks = jax.random.split(key, 9)
        s = 0.02
        x = jax.random.normal(ks[0], (4, 256, DMODEL), dtype=jnp.float32)
        Wq = jax.random.normal(ks[1], (DMODEL, DMODEL), dtype=jnp.float32) * s
        bq = jax.random.normal(ks[2], (DMODEL,), dtype=jnp.float32) * s
        Wk = jax.random.normal(ks[3], (DMODEL, DMODEL), dtype=jnp.float32) * s
        bk = jax.random.normal(ks[4], (DMODEL,), dtype=jnp.float32) * s
        Wv = jax.random.normal(ks[5], (DMODEL, DMODEL), dtype=jnp.float32) * s
        bv = jax.random.normal(ks[6], (DMODEL,), dtype=jnp.float32) * s
        Wo = jax.random.normal(ks[7], (DMODEL, DMODEL), dtype=jnp.float32) * s
        bo = jax.random.normal(ks[8], (DMODEL,), dtype=jnp.float32) * s
        return {'x': x, 'Wq': Wq, 'bq': bq, 'Wk': Wk, 'bk': bk, 'Wv': Wv, 'bv': bv, 'Wo': Wo, 'bo': bo}
    _L0_attn_in = _L0_attn_setup()

    def _L0_ffn_setup():
        import jax, jax.numpy as jnp
        import numpy as np
        NUM_EXPERTS = 8
        TOP_K = 2
        EMB = 256
        MLP = 512
        B, S = (4, 128)
        key = jax.random.key(seed)
        ks = jax.random.split(key, 5)
        scale_x = 1.0
        return {'x': jax.random.normal(ks[0], (B, S, EMB), dtype=jnp.float32), 'gate_kernel': jax.random.normal(ks[1], (EMB, NUM_EXPERTS), dtype=jnp.float32) / np.sqrt(EMB), 'w0_kernel': jax.random.normal(ks[2], (NUM_EXPERTS, EMB, MLP), dtype=jnp.float32) / np.sqrt(EMB), 'w1_kernel': jax.random.normal(ks[3], (NUM_EXPERTS, EMB, MLP), dtype=jnp.float32) / np.sqrt(EMB), 'wo_kernel': jax.random.normal(ks[4], (NUM_EXPERTS, MLP, EMB), dtype=jnp.float32) / np.sqrt(MLP)}
    _L0_ffn_in = _L0_ffn_setup()
    _L0_c = _w((lambda *s: np.random.randn(*s).astype(np.float32) * 0.05)(4, 256))
    _L0_wmod = _w((lambda *s: np.random.randn(*s).astype(np.float32) * 0.05)(256, 6 * 256) * 256 ** (-0.5))
    _d = {'L0_attn_x': _L0_attn_in['x'], 'L0_attn_Wq': _L0_attn_in['Wq'], 'L0_attn_bq': _L0_attn_in['bq'], 'L0_attn_Wk': _L0_attn_in['Wk'], 'L0_attn_bk': _L0_attn_in['bk'], 'L0_attn_Wv': _L0_attn_in['Wv'], 'L0_attn_bv': _L0_attn_in['bv'], 'L0_attn_Wo': _L0_attn_in['Wo'], 'L0_attn_bo': _L0_attn_in['bo'], 'L0_ffn_gate_kernel': _L0_ffn_in['gate_kernel'], 'L0_ffn_w0_kernel': _L0_ffn_in['w0_kernel'], 'L0_ffn_w1_kernel': _L0_ffn_in['w1_kernel'], 'L0_ffn_wo_kernel': _L0_ffn_in['wo_kernel'], 'L0_c': _L0_c, 'L0_wmod': _L0_wmod}
    _x0 = _d['L0_attn_x']
    _d['L0_attn_x'] = jax.random.normal(jax.random.fold_in(jax.random.key(seed), 1), (4, 256, 256), dtype=_x0.dtype)
    del _x0
    return _d

def reference(L0_attn_x, L0_attn_Wq, L0_attn_bq, L0_attn_Wk, L0_attn_bk, L0_attn_Wv, L0_attn_bv, L0_attn_Wo, L0_attn_bo, L0_ffn_gate_kernel, L0_ffn_w0_kernel, L0_ffn_w1_kernel, L0_ffn_wo_kernel, L0_c, L0_wmod):

    def _L0_attn_ref(x, Wq, bq, Wk, bk, Wv, bv, Wo, bo):
        import jax, jax.numpy as jnp
        import numpy as np
        DMODEL = 256
        HEADS = 16
        DHEAD = DMODEL // HEADS
        b, l, _ = x.shape
        q = (x @ Wq + bq).reshape(b, l, HEADS, DHEAD)
        k = (x @ Wk + bk).reshape(b, l, HEADS, DHEAD)
        v = (x @ Wv + bv).reshape(b, l, HEADS, DHEAD)
        a = jnp.einsum('blhd,bLhd->bhlL', q, k) * (1.0 / DHEAD)
        a = jax.nn.softmax(a, axis=-1)
        prefinal = jnp.einsum('bhlL,bLhd->blhd', a, v)
        out = prefinal.reshape(b, l, HEADS * DHEAD) @ Wo + bo
        return out

    def _L0_ffn_ref(x, gate_kernel, w0_kernel, w1_kernel, wo_kernel):
        import jax, jax.numpy as jnp
        import numpy as np
        NUM_EXPERTS = 8
        TOP_K = 2
        EMB = 256
        MLP = 512
        B, S = (4, 128)
        gate_logits = jnp.einsum('bsd,de->bse', x, gate_kernel)
        top_k_weights, top_k_indices = jax.lax.top_k(gate_logits, TOP_K)
        top_k_weights = jax.nn.softmax(top_k_weights.astype(jnp.float32), axis=-1).astype(x.dtype)
        one_hot = jax.nn.one_hot(top_k_indices, NUM_EXPERTS, dtype=x.dtype)
        combine = jnp.einsum('bsk,bske->bse', top_k_weights, one_hot)
        h0 = jnp.einsum('bsd,edm->bsem', x, w0_kernel)
        h1 = jnp.einsum('bsd,edm->bsem', x, w1_kernel)
        inter = jax.nn.silu(h0) * h1
        out = jnp.einsum('bse,bsem,emd->bsd', combine, inter, wo_kernel)
        return out
    x = L0_attn_x
    mod = (_silu(L0_c) @ L0_wmod).reshape(L0_c.shape[0], 6, 1, -1)
    sa, ca, ga, sb, cb, gb = (mod[:, 0], mod[:, 1], mod[:, 2], mod[:, 3], mod[:, 4], mod[:, 5])
    ga = (2 * (ga >= 0) - 1) * jnp.maximum(jnp.abs(ga), 0.25)
    gb = (2 * (gb >= 0) - 1) * jnp.maximum(jnp.abs(gb), 0.25)
    h = _layernorm(x, axis=-1) * (1 + ca) + sa
    x = x + ga * _L0_attn_ref(h, L0_attn_Wq, L0_attn_bq, L0_attn_Wk, L0_attn_bk, L0_attn_Wv, L0_attn_bv, L0_attn_Wo, L0_attn_bo)
    h = _layernorm(x, axis=-1) * (1 + cb) + sb
    x = x + gb * _L0_ffn_ref(h, L0_ffn_gate_kernel, L0_ffn_w0_kernel, L0_ffn_w1_kernel, L0_ffn_wo_kernel)
    return x

_drawn_inputs = setup_inputs


def setup_inputs(seed=0):
    import zlib

    import numpy as np

    out = dict(_drawn_inputs(seed))
    spreads = {}
    factors = {'L0_attn_Wq': 8.0,
     'L0_attn_bq': 8.0,
     'L0_attn_Wk': 8.0,
     'L0_attn_bk': 8.0,
     'L0_attn_Wv': 8.0,
     'L0_attn_bv': 8.0,
     'L0_attn_Wo': 8.0,
     'L0_attn_bo': 7.72}
    for name, (base, spread) in spreads.items():
        noise = np.random.default_rng([zlib.crc32(name.encode()), seed]).standard_normal(out[name].shape)
        drawn = base * np.exp(spread * noise) if base else spread * noise
        out[name] = jnp.asarray(drawn.astype(out[name].dtype))
    for name, factor in factors.items():
        out[name] = (out[name] * factor).astype(out[name].dtype)
    return out
```

```python
from contextlib import ExitStack

import concourse.bass as bass
from concourse import mybir

F32 = mybir.dt.float32
F32R = mybir.dt.float32r
BF16 = mybir.dt.bfloat16
I32 = mybir.dt.int32
U32 = mybir.dt.uint32
ALU = mybir.AluOpType
ACT = mybir.ActivationFunctionType
AX = mybir.AxisListType

P = 128
B, L, D = 4, 256, 256
HEADS, DH = 16, 16
NE, F = 8, 512
KC = D // P
QT = L // P
T = B * QT
NG = HEADS // 2
HR = 64
K_MAX = 3 * DH
K_SUB = K_MAX + 2
FC = F // P
NT = (2 * B * L + NE * (P - 1)) // P
TOK, E1, W2, DW = range(4)
EPS = 1e-5


def adaln_block(nc, x, wq, bq, wk, bk, wv, bv, wo, bo, gate, w0, w1, wout, cT, wmod, out):
    ctx = ExitStack()
    with ctx:
        top = [16512]

        def at(name, shape, dt, offset):
            return nc.alloc_sbuf_tensor_at(name, shape, dt, offset=offset)

        def sb(name, shape, dt):
            n = 4 if dt != BF16 else 2
            for s in shape[1:]:
                n *= s
            t = at(name, shape, dt, top[0])
            top[0] += (n + 31) // 32 * 32
            return t

        def sem(name):
            return ctx.enter_context(nc.semaphore(name))

        w01 = sb("w01", [P, NE, KC, 2 * F], F32)
        late = top[0]
        wex = sb("wex", [P, NE, FC, D], F32)
        probs = at("probs", [P, 4, 2, QT * L], F32, late)
        wmod_sb = at("wmod_sb", [P, KC, 6 * D], F32, late + 16384)
        h1n = at("h1n", [P, QT, D], F32, late + 28672)
        hT = at("hT", [P, KC, L], F32, late + 30720)
        xs = sb("xs", [P, T, D], F32)
        gates = sb("gates", [P, 4, B, D], F32)
        w_raw = at("w_raw", [P, 4, KC, D], F32, top[0] - 8192)
        GA, SBI, CB1, GB = range(4)
        bv_b = sb("bv_b", [P, D], F32)
        bo_b = sb("bo_b", [P, D], F32)
        gbo = sb("gbo", [P, D], F32)
        ident = sb("ident", [P, P], F32)
        bqk = sb("bqk", [P, 2, KC], F32)
        gate_sb = sb("gate_sb", [P, KC, NE], F32)
        cT_sb = sb("cT_sb", [P, KC, B], F32)
        sc = sb("sc", [P, KC, B], F32)
        modT = sb("modT", [P, 4, B], F32)
        mrow = sb("mrow", [P, 2 * D], F32)
        gsign = at("gsign", [P, D], F32, late + 16384)
        gabs = at("gabs", [P, D], F32, late + 17408)
        stats = sb("stats", [P, QT, 6], F32)
        mv = sb("mv", [P, 2, T, 2], F32)
        veps = sb("veps", [P, 2, T], F32)
        rstd = sb("rstd", [P, 2, T], F32)
        mhalf = sb("mhalf", [P, QT], F32)
        mx = sb("mx", [P, 2, QT, HEADS], F32)
        attn_top = top[0]
        whi = sb("whi", [P, 4, KC, D], F32R)
        wlo = sb("wlo", [P, 4, KC, D], F32R)
        qs = sb("qs", [P, 2, NG, L], F32R)
        ks = sb("ks", [P, 2, NG, L], F32R)
        va = sb("va", [P, 3, QT, HEADS, 32], F32)
        hhi = sb("hhi", [P, KC, L], F32R)
        hlo = sb("hlo", [P, KC, L], F32R)
        qk = sb("qk", [P, 4, KC, L], F32R)
        mneg = sb("mneg", [HEADS, 2, L], F32R)
        oT = at("oT", [P, HEADS // 4, L], F32, late + 16384)
        on = at("on", [P, QT, D], F32, late + 20480)
        ohi = at("ohi", [P, KC, L], F32R, late + 22528)
        olo = at("olo", [P, KC, L], F32R, late + 24576)
        rden = sb("rden", [P, HEADS], F32)
        h2r = sb("h2r", [P, QT, D], F32)
        info = sb("info", [P, QT, 4], F32)
        pad_info = sb("pad_info", [P, 4], F32)
        h2T = sb("h2T", [P, KC, L], F32)
        iota8 = sb("iota8", [P, NE], F32)
        region = sb("region", [P, NE], F32)
        steps = sb("steps", [P, NE], F32)
        ones8 = sb("ones8", [P, NE], F32)
        tile_no = sb("tile_no", [P, NT], F32)
        tile_row = sb("tile_row", [P, NT], F32)
        token = sb("token", [P, T], F32)
        pad_row = sb("pad_row", [P, 1], F32)
        upper = sb("upper", [P, P], BF16)
        ones_bf = sb("ones_bf", [P, P], BF16)
        lg = sb("lg", [P, QT, NE], F32)
        m8 = sb("m8", [P, QT, 8], F32)
        i8 = sb("i8", [P, QT, 8], U32)
        dlt = sb("dlt", [P, QT], F32)
        edlt = sb("edlt", [P, QT], F32)
        wsum = sb("wsum", [P, QT], F32)
        e12 = sb("e12", [P, QT, 2], F32)
        hot = sb("hot", [P, QT, 2, NE], F32)
        picked = sb("picked", [P, T, NE], BF16)
        pos = sb("pos", [P, QT, NE], F32)
        slotf = sb("slotf", [P, QT, 2], F32)
        slot = sb("slot", [P, QT, 2], U32)
        count = sb("count", [P, NE], F32)
        tiles = sb("tiles", [P, NE], F32)
        tend = sb("tend", [P, NE], F32)
        tbeg = sb("tbeg", [P, NE], F32)
        assert top[0] <= nc.sbuf_usable_end, top[0]
        top[0] = attn_top
        pick = sb("pick", [P, NT, NE], F32)
        prod = sb("prod", [P, NT, NE], F32)
        texp = sb("texp", [P, NT], F32)
        tbase = sb("tbase", [P, NT], F32)
        tcount = sb("tcount", [P, NT], F32)
        trow = sb("trow", [P, NT], F32)
        valid = sb("valid", [P, NT], F32)
        gidx = sb("gidx", [P, NT], U32)
        texp_i = sb("texp_i", [P, NT], I32)
        gcur = [sb(f"gcur{i}", [P, 1], U32) for i in range(2)]
        ecur = [sb(f"ecur{i}", [P, 1], F32) for i in range(2)]
        tok = [sb(f"tok{i}", [P, 1], U32) for i in range(2)]
        wgt = [sb(f"wgt{i}", [P, 1], F32) for i in range(2)]
        wtmp = [sb(f"wtmp{i}", [P, 1], F32) for i in range(2)]
        tokg = [sb(f"tokg{i}", [P, 1], U32) for i in range(2)]
        inf = [sb(f"inf{i}", [P, 4], F32) for i in range(2)]
        xg = [sb(f"xg{i}", [P, D], F32) for i in range(2)]
        xT = [sb(f"xT{i}", [P, KC, P], F32) for i in range(2)]
        act0 = [sb(f"act0{i}", [P, F], F32) for i in range(2)]
        inter = [sb(f"inter{i}", [P, F], F32) for i in range(2)]
        iT = [sb(f"iT{i}", [P, FC, P], F32) for i in range(2)]
        ys = [sb(f"ys{i}", [P, D], F32) for i in range(2)]
        acc = sb("acc", [P, T, D], F32)
        assert top[0] <= nc.sbuf_usable_end, top[0]

        ps_s = [ctx.enter_context(nc.psum_tensor(f"ps_s{i}", [P, 2, L], F32)) for i in range(2)]
        ps_t = [ctx.enter_context(nc.psum_tensor(f"ps_t{i}", [P, 2, QT * L], F32)) for i in range(2)]
        ps_pv = ctx.enter_context(nc.psum_tensor("ps_pv", [P, 2, L], F32))
        ps_w = ctx.enter_context(nc.psum_tensor("ps_w", [P, 512], F32))
        ps_qk = [ps_t[0][:, i, :].rearrange("p (m t) -> p m t", m=KC) for i in range(2)]
        ps_v = ps_t[1][:, 0, :].rearrange("p (t n) -> p t n", t=QT)
        ps_wk = ps_w[:].rearrange("p (k t) -> p k t", k=2)
        ps_h = ps_t
        ps_x = ps_w[:, 0:KC * P].rearrange("p (k t) -> p k t", k=KC)
        ps_i = ps_pv[:].rearrange("p a b -> p (a b)")
        ps_y = [ps_s[i][:, 0, :] for i in range(2)]

        info_d = nc.dram_tensor("routed", (NE * B * L + P, 4), F32, kind="Internal").ap()
        h2_d = nc.dram_tensor("h2_rows", (B * L + P, D), F32, kind="Internal").ap()
        acc_d = nc.dram_tensor("mixture_sums", (B * L + P, D), F32, kind="Internal").ap()
        scratch = nc.dram_tensor("qk_scratch", (B, 4, D, L), F32, kind="Internal").ap()
        mod_d = nc.dram_tensor("mod_scratch", (4, B, D), F32, kind="Internal").ap()

        x_in = [sem(f"x_in{b}") for b in range(B)]
        c_in = sem("c_in")
        wmod_in = sem("wmod_in")
        wraw_in = sem("wraw_in")
        small_in = sem("small_in")
        ident_ok = sem("ident_ok")
        zero_ok = sem("zero_ok")
        ones_ok = sem("ones_ok")
        dve_chain = sem("dve_chain")
        pool_chain = sem("pool_chain")
        silu_ok = sem("silu_ok")
        mod_ps = sem("mod_ps")
        mrow_ok = sem("mrow_ok")
        modT_ps = sem("modT_ps")
        modT_ok = sem("modT_ok")
        mod_out = sem("mod_out")
        gates_in = sem("gates_in")
        wsplit_ok = sem("wsplit_ok")
        var_ok = sem("var_ok")
        rstd_ok = sem("rstd_ok")
        h1n_ok = sem("h1n_ok")
        hT_ps = sem("hT_ps")
        hT_ok = sem("hT_ok")
        h_ok = sem("h_ok")
        q_ps = sem("q_ps")
        k_ps = sem("k_ps")
        v_ps = sem("v_ps")
        qhi_ok = sem("qhi_ok")
        khi_ok = sem("khi_ok")
        qlo_ok = sem("qlo_ok")
        klo_ok = sem("klo_ok")
        va_ok = sem("va_ok")
        qk_out = [sem(f"qk_out{p}") for p in range(2)]
        stack_in = [sem(f"stack_in{p}") for p in range(2)]
        s_ps = sem("s_ps")
        mx_ok = sem("mx_ok")
        mT_ps = sem("mT_ps")
        mhi_ok = sem("mhi_ok")
        mlo_ok = sem("mlo_ok")
        m_in = [sem(f"m_in{p}") for p in range(2)]
        t_ps = sem("t_ps")
        exp_ok = sem("exp_ok")
        pv_ps = sem("pv_ps")
        oT_ok = sem("oT_ok")
        tr1_ps = sem("tr1_ps")
        on_ok = sem("on_ok")
        tr2_ps = sem("tr2_ps")
        ohi_ok = sem("ohi_ok")
        olo_ok = sem("olo_ok")
        wo_ps = sem("wo_ps")
        xb_ok = sem("xb_ok")
        x2_ok = sem("x2_ok")
        w01_in = sem("w01_in")
        wex_in = sem("wex_in")
        pad_ok = sem("pad_ok")
        pad_out = sem("pad_out")
        const_ok = sem("const_ok")
        h2n_ok = sem("h2n_ok")
        h2_ok = sem("h2_ok")
        h2T_ps = sem("h2T_ps")
        h2T_ok = sem("h2T_ok")
        lg_ps = sem("lg_ps")
        lg_ok = sem("lg_ok")
        dlt_ok = sem("dlt_ok")
        edlt_ok = sem("edlt_ok")
        picked_ok = sem("picked_ok")
        rank_ps = sem("rank_ps")
        slot_ok = sem("slot_ok")
        routed = sem("routed")
        count_ps = sem("count_ps")
        plan_ok = sem("plan_ok")
        xg_in = [sem(f"xg_in{i}") for i in range(2)]
        x_ps = sem("x_ps")
        xT_ok = sem("xT_ok")
        hid_ps = sem("hid_ps")
        act0_ok = sem("act0_ok")
        inter_ok = sem("inter_ok")
        i_ps = sem("i_ps")
        cur_ok = sem("cur_ok")
        tokg_ok = sem("tokg_ok")
        inf_in = [sem(f"inf_in{i}") for i in range(2)]
        h2_out = sem("h2_out")
        zeros_out = sem("zeros_out")
        pool_waited = sem("pool_waited")
        tok_ok = sem("tok_ok")
        wtmp_ok = sem("wtmp_ok")
        pos_ok = sem("pos_ok")
        iT_ok = sem("iT_ok")
        y_ps = sem("y_ps")
        wgt_ok = sem("wgt_ok")
        ys_ok = sem("ys_ok")
        y_added = [sem(f"y_added{i}") for i in range(2)]
        acc_in = [sem(f"acc_in{b}") for b in range(B)]
        res_ok = sem("res_ok")
        out_done = sem("out_done")

        def landed(b):
            return 64 * (b // 2 + 1)

        block = ctx.enter_context(nc.Block())

        @block.sync
        def _(sp):
            def rows(w):
                return w.rearrange("(k p) n -> p k n", p=P)

            sp.dma_start(cT_sb[:], rows(cT)).then_inc(c_in, 16)
            for b in range(B):
                sp.dma_start(xs[:, QT * b:QT * b + QT, :],
                             x[b].rearrange("(t p) d -> p t d", p=P)).then_inc(x_in[b], 16)
                if b == 0:
                    for k in range(KC):
                        sp.dma_start(wmod_sb[:, k, :], wmod[P * k:P * k + P, :]).then_inc(wmod_in, 16)
                    for i, w in enumerate((wq, wk, wv, wo)):
                        sp.dma_start(w_raw[:, i], rows(w)).then_inc(wraw_in, 16)
                    sp.dma_start(bqk[:, 0, :], bq).then_inc(small_in, 16)
                    sp.dma_start(bqk[:, 1, :], bk).then_inc(small_in, 16)
                    sp.dma_start(bv_b[:], bv.partition_broadcast(P)).then_inc(small_in, 16)
                    sp.dma_start(bo_b[:], bo.partition_broadcast(P)).then_inc(small_in, 16)
                    sp.dma_start(gate_sb[:], rows(gate)).then_inc(small_in, 16)

            sp.wait_ge(pad_ok, 2)
            sp.dma_start(acc_d.rearrange("(t p) d -> p t d", p=P),
                         h2T[:, 0, :].unsqueeze(1).broadcast_to([P, T + 1, D])).then_inc(pad_out, 16)
            sp.dma_start(h2_d[B * L:B * L + P], h2T[:, 0, :]).then_inc(pad_out, 16)
            n = (NE * B * L + P) * 4 // P
            sp.dma_start(info_d.rearrange("(p r) c -> p (r c)", p=P),
                         h2T[:].rearrange("p k t -> p (k t)")[:, 0:n]).then_inc(zeros_out, 16)
            sp.wait_ge(zeros_out, 16)
            sp.dma_start(info_d[NE * B * L:NE * B * L + P], pad_info[:]).then_inc(pad_out, 16)

            sp.wait_ge(mrow_ok, 3)
            for i, (r, c) in ((GA, (32, 0)), (SBI, (32, D)), (CB1, (64, 0)), (GB, (64, D))):
                sp.dma_start(mod_d[i], mrow[r:r + B, c:c + D]).then_inc(mod_out, 16)
            sp.wait_ge(mod_out, 64)
            sp.wait_ge(wsplit_ok, 2)
            for i in range(4):
                sp.dma_start(gates[:, i], mod_d[i].partition_broadcast(P)).then_inc(gates_in, 16)

            def stack(b):
                p = b % 2
                for i, ready in enumerate((qhi_ok, qlo_ok, khi_ok, klo_ok)):
                    sp.wait_ge(ready, b + 1)
                    sp.dma_start(scratch[b, i].rearrange("(m p) t -> p m t", p=P),
                                 qk[:, i].bitcast(F32)).then_inc(qk_out[p], 16)
                sp.wait_ge(qk_out[p], landed(b))
                if b >= 2:
                    sp.wait_ge(t_ps, NG * (b - 1))
                else:
                    sp.wait_ge(ones_ok, 2 + p)
                for s in range(3):
                    for dst, kinds in ((qs, (0, 0, 1)), (ks, (2, 3, 2))):
                        src = scratch[b, kinds[s]].rearrange("(g h d) t -> h d g t", g=NG, h=2)
                        for hp in range(2):
                            r = HR * hp + DH * s
                            sp.dma_start(dst[r:r + DH, p, :, :].bitcast(F32), src[hp]).then_inc(stack_in[p], 16)

            def maxima(b):
                p = b % 2
                sp.wait_ge(mhi_ok, b + 1)
                sp.wait_ge(mlo_ok, b + 1)
                for hp in range(2):
                    for i in range(2):
                        r = HR * hp + K_MAX + i
                        sp.dma_start(qs[r:r + 1, p, :, :].bitcast(F32),
                                     mneg[NG * hp:NG * hp + NG, i, :].bitcast(F32)).then_inc(m_in[p], 16)

            def experts(first, n):
                for e in range(first, first + n):
                    for i, w in enumerate((w0, w1)):
                        sp.dma_start(w01[:, e, :, F * i:F * i + F], rows(w[e])).then_inc(w01_in, 16)

            stack(0)
            stack(1)
            maxima(0)
            for b in range(B):
                if b + 2 < B:
                    stack(b + 2)
                experts(2 * b, 2)
                if b + 1 < B:
                    maxima(b + 1)
            sp.wait_ge(x2_ok, B)
            for e in range(NE):
                sp.dma_start(wex[:, e], wout[e].rearrange("(m p) d -> p m d", p=P)).then_inc(wex_in, 16)
            sp.wait_ge(y_added[0], 16 * ((NT + 1) // 2))
            sp.wait_ge(y_added[1], 16 * (NT // 2))
            for b in range(B):
                sp.dma_start(acc[:, QT * b:QT * b + QT, :],
                             acc_d[L * b:L * b + L].rearrange("(t p) d -> p t d", p=P)).then_inc(acc_in[b], 16)
            for b in range(B):
                sp.wait_ge(res_ok, b + 1)
                sp.dma_start(out[b].rearrange("(t p) d -> p t d", p=P),
                             acc[:, QT * b:QT * b + QT, :]).then_inc(out_done, 16)
            sp.wait_ge(out_done, 16 * B)

        @block.gpsimd
        def _(pool):
            chain = [0]

            def link(ins):
                chain[0] += 1
                ins.then_inc(pool_chain, 1)
                pool.wait_ge(pool_chain, chain[0])

            link(nc.gpsimd.memset(ident[:], 0.0))
            nc.gpsimd.affine_select(out=ident[:], in_=ident[:], compare_op=ALU.not_equal, fill=1.0, base=0,
                                    pattern=[[-1, P]], channel_multiplier=1).then_inc(ident_ok, 1)
            link(nc.gpsimd.memset(mhalf[:], -0.5))
            nc.gpsimd.memset(va[:], 1.0).then_inc(ones_ok, 1)
            for p in range(2):
                nc.gpsimd.memset(ks[:, p].bitcast(F32), 1.0).then_inc(ones_ok, 1)

            for t, pattern, base, mult in ((iota8[:], [[1, NE]], 0, 0), (region[:], [[B * L, NE]], 0, 0),
                                           (steps[:], [[P, NE]], 0, 0), (tile_no[:], [[1, NT]], 0, 0),
                                           (tile_row[:], [[P, NT]], 0, 1), (token[:], [[P, T]], 0, 1),
                                           (pad_row[:], [[0, 1]], NE * B * L, 1)):
                nc.gpsimd.iota(t, pattern, base=base, channel_multiplier=mult, allow_small_or_imprecise_dtypes=True)
            link(nc.gpsimd.memset(upper[:], 1.0))
            nc.gpsimd.affine_select(out=upper[:], in_=upper[:], compare_op=ALU.is_gt, fill=0.0, base=0,
                                    pattern=[[1, P]], channel_multiplier=-1)
            nc.gpsimd.memset(ones8[:], 1.0)
            nc.gpsimd.memset(ones_bf[:], 1.0).then_inc(const_ok, 1)
            link(nc.gpsimd.memset(pad_info[:], 0.0))
            nc.gpsimd.iota(pad_info[:, TOK:TOK + 1], [[0, 1]], base=B * L, channel_multiplier=1,
                           allow_small_or_imprecise_dtypes=True).then_inc(pad_ok, 1)
            nc.gpsimd.memset(h2T[:], 0.0).then_inc(pad_ok, 1)

            def rsqrt(ln, b):
                pool.wait_ge(var_ok, B * ln + b + 1)
                s = slice(QT * b, QT * b + QT)
                nc.gpsimd.tensor_tensor(rstd[:, ln, s], veps[:, ln, s], mhalf[:], ALU.pow).then_inc(rstd_ok, 1)

            for b in range(B):
                rsqrt(0, b)
            pool.wait_ge(gates_in, 64)
            pool.wait_ge(small_in, 80)
            for b in range(B):
                link(nc.gpsimd.tensor_tensor(gbo[:], bo_b[:], gates[:, GA, b, :], ALU.mult))
                pool.wait_ge(h1n_ok, b + 1)
                for t in range(QT):
                    last = nc.gpsimd.tensor_tensor(xs[:, QT * b + t, :], xs[:, QT * b + t, :], gbo[:], ALU.add)
                    link(last)
                pool.sem_inc(xb_ok, 1)

            def modulate(b):
                rsqrt(1, b)
                pool.wait_ge(h2n_ok, b + 1)
                h = h2r[:]
                for i, op in ((CB1, ALU.mult), (SBI, ALU.add)):
                    g = gates[:, i, b, :].unsqueeze(1).broadcast_to([P, QT, D])
                    last = nc.gpsimd.tensor_tensor(h, h, g, op)
                    if op == ALU.mult:
                        link(last)
                last.then_inc(h2_ok, 1)
                pool.wait_ge(h2_ok, b + 1)
                pool.dma_start(h2_d[L * b:L * b + L].rearrange("(t p) d -> p t d", p=P), h).then_inc(h2_out, 16)

            def route(b):
                pool.wait_ge(slot_ok, b + 1)
                if b == 0:
                    pool.wait_ge(pad_out, 48)
                for t in range(QT):
                    for c in range(2):
                        nc.gpsimd.indirect_dma_start(
                            out=info_d, out_offset=bass.IndirectOffsetOnAxis(ap=slot[:, t, c:c + 1], axis=0),
                            in_=info[:, t, :], in_offset=None).then_inc(routed, 16)

            for b in range(B):
                modulate(b)
                route(b)

            def apart():
                pool.sem_inc(pool_waited, 1)

            def fetch(j, par):
                nc.gpsimd.tensor_copy(gcur[par][:], gidx[:, bass.ds(j, 1)]).then_inc(cur_ok, 1)
                nc.gpsimd.tensor_copy(ecur[par][:], texp[:, bass.ds(j, 1)]).then_inc(cur_ok, 1)
                pool.wait_ge(cur_ok, 2 * j + 2)
                apart()
                nc.gpsimd.indirect_dma_start(
                    out=inf[par][:], out_offset=None, in_=info_d,
                    in_offset=bass.IndirectOffsetOnAxis(ap=gcur[par][:], axis=0)).then_inc(inf_in[par], 16)

            def gather(i, par, wait=True):
                j = 2 * i + par
                pool.wait_ge(inf_in[par], 16 * i + 16)
                apart()
                nc.gpsimd.tensor_copy(tokg[par][:], inf[par][:, TOK:TOK + 1]).then_inc(tokg_ok, 1)
                pool.wait_ge(tokg_ok, j + 1)
                if wait:
                    pool.wait_ge(x_ps, j - 1)
                apart()
                nc.gpsimd.indirect_dma_start(
                    out=xg[par][:], out_offset=None, in_=h2_d,
                    in_offset=bass.IndirectOffsetOnAxis(ap=tokg[par][:], axis=0)).then_inc(xg_in[par], 16)

            def weigh(i, par):
                j = 2 * i + par
                g = inf[par]
                nc.gpsimd.tensor_copy(tok[par][:], g[:, TOK:TOK + 1]).then_inc(tok_ok, 1)
                nc.gpsimd.tensor_scalar(wtmp[par][:], g[:, E1:E1 + 1], ecur[par][:], g[:, DW:DW + 1],
                                        ALU.is_equal, ALU.mult).then_inc(wtmp_ok, 1)
                pool.wait_ge(wtmp_ok, j + 1)
                apart()
                nc.gpsimd.tensor_tensor(wgt[par][:], wtmp[par][:], g[:, W2:W2 + 1], ALU.add).then_inc(wgt_ok, 1)

            def add_rows(i, par):
                j = 2 * i + par
                pool.wait_ge(ys_ok, j + 3)
                pool.wait_ge(tok_ok, j + 1)
                if not isinstance(i, int) or i + par:
                    pool.wait_ge(y_added[1 - par], 16 * i + 16 * par)
                apart()
                nc.gpsimd.indirect_dma_start(
                    out=acc_d, out_offset=bass.IndirectOffsetOnAxis(ap=tok[par][:], axis=0),
                    in_=ys[par][:], in_offset=None, compute_op=ALU.add).then_inc(y_added[par], 16)

            pool.wait_ge(routed, 64 * B)
            pool.wait_ge(h2_out, 16 * B)
            pool.wait_ge(plan_ok, 1)
            fetch(0, 0)
            fetch(1, 1)
            gather(0, 0, wait=False)
            gather(0, 1, wait=False)
            weigh(0, 0)
            fetch(2, 0)
            n = (NT - 3) // 2

            def two_tiles(i):
                for par in range(2):
                    gather(i + 1, par)
                    add_rows(i, par)
                    weigh(i + par, 1 - par)
                    fetch(2 * i + par + 3, 1 - par)

            two_tiles(0)
            with pool.Fori(1, n) as i:
                two_tiles(i)
            gather(n + 1, 0)
            add_rows(n, 0)
            weigh(n, 1)
            add_rows(n, 1)
            weigh(n + 1, 0)
            add_rows(n + 1, 0)

        @block.scalar
        def _(act):
            act.wait_ge(c_in, 16)
            nc.scalar.activation(sc[:], cT_sb[:], ACT.Silu).then_inc(silu_ok, 1)

            def project(b):
                act.wait_ge(hT_ps, b + 1)
                act.wait_ge(modT_ok, 1)
                if b:
                    act.wait_ge(h_ok, b)
                for k in range(KC):
                    nc.scalar.activation(hT[:, k, :], ps_wk[:, k, :], ACT.Identity, scale=modT[:, 2 + k, b:b + 1],
                                         bias=modT[:, k, b:b + 1]).then_inc(hT_ok, 1)
                act.wait_ge(small_in, 80)
                for i, (done, ready) in enumerate(((q_ps, qhi_ok), (k_ps, khi_ok))):
                    act.wait_ge(done, b + 1)
                    if b:
                        act.wait_ge(qk_out[(b - 1) % 2], landed(b - 1))
                    for m in range(KC):
                        last = nc.scalar.activation(qk[:, 2 * i, m, :], ps_qk[i][:, m, :], ACT.Identity,
                                                    bias=bqk[:, i, m:m + 1])
                    last.then_inc(ready, 1)

            def maxima(b):
                act.wait_ge(mT_ps, b + 1)
                if b:
                    act.wait_ge(m_in[(b - 1) % 2], landed(b - 1))
                nc.scalar.activation(mneg[:, 0, :], ps_w[0:HEADS, 0:L], ACT.Copy, scale=-1.0).then_inc(mhi_ok, 1)

            def exponentials(b, g):
                u = NG * b + g
                act.wait_ge(t_ps, u + 1)
                if u >= 4:
                    act.wait_ge(pv_ps, u // 2 - 1)
                nc.scalar.activation(probs[:, g % 4], ps_t[g % 2][:], ACT.Exp, scale=1.0 / DH).then_inc(exp_ok, 1)

            def keep_o(b, half):
                act.wait_ge(pv_ps, 4 * b + 2 * half + 2)
                if b:
                    act.wait_ge(tr1_ps, QT * b)
                nc.scalar.activation(oT[:, 2 * half:2 * half + 2, :], ps_pv[:], ACT.Copy).then_inc(oT_ok, 1)

            def split_o(b):
                act.wait_ge(tr2_ps, b + 1)
                if b:
                    act.wait_ge(wo_ps, b)
                nc.scalar.activation(ohi[:], ps_wk, ACT.Copy).then_inc(ohi_ok, 1)

            def keep_h2T(b):
                act.wait_ge(h2T_ps, b + 1)
                if b:
                    act.wait_ge(lg_ps, b)
                else:
                    act.wait_ge(pad_out, 48)
                nc.scalar.activation(h2T[:], ps_wk, ACT.Copy).then_inc(h2T_ok, 1)

            def exp_gap(b):
                act.wait_ge(dlt_ok, b + 1)
                nc.scalar.activation(edlt[:], dlt[:], ACT.Exp).then_inc(edlt_ok, 1)

            project(0)
            project(1)
            maxima(0)
            for b in range(B):
                if b + 2 < B:
                    project(b + 2)
                for g in range(NG):
                    exponentials(b, g)
                    if g == 3 and b >= 2:
                        keep_h2T(b - 2)
                    if g == 4 and b:
                        split_o(b - 1)
                    if g == 5:
                        keep_o(b, 0)
                    if g == 6 and b >= 2:
                        exp_gap(b - 2)
                keep_o(b, 1)
                if b + 1 < B:
                    maxima(b + 1)
            keep_h2T(B - 2)
            exp_gap(B - 2)
            split_o(B - 1)
            keep_h2T(B - 1)
            exp_gap(B - 1)

            def keep_x(i, par):
                j = 2 * i + par
                act.wait_ge(x_ps, j + 1)
                nc.scalar.activation(xT[par][:], ps_x, ACT.Copy).then_inc(xT_ok, 1)

            def silu(i, par):
                j = 2 * i + par
                act.wait_ge(hid_ps, j + 1)
                act.wait_ge(inter_ok, j + 1)
                nc.scalar.activation(act0[par][:], ps_h[par][:, 0, :], ACT.Silu).then_inc(act0_ok, 1)

            def scale_y(i, par):
                j = 2 * i + par
                act.wait_ge(y_ps, j + 1)
                act.wait_ge(wgt_ok, j + 1)
                if not isinstance(i, int) or i:
                    act.wait_ge(y_added[par], 16 * i)
                nc.scalar.activation(ys[par][:], ps_y[par], ACT.Copy, scale=wgt[par][:]).then_inc(ys_ok, 1)

            act.sem_inc(ys_ok, 2)
            keep_x(0, 0)
            keep_x(0, 1)
            silu(0, 0)
            n = (NT - 3) // 2

            def two_tiles(i):
                for par in range(2):
                    silu(i + par, 1 - par)
                    scale_y(i, par)
                    keep_x(i + 1, par)

            two_tiles(0)
            with act.Fori(1, n) as i:
                two_tiles(i)
            silu(n, 1)
            scale_y(n, 0)
            keep_x(n + 1, 0)
            silu(n + 1, 0)
            scale_y(n, 1)
            scale_y(n + 1, 0)

        @block.vector
        def _(dve):
            chain = [0]

            def link(ins):
                chain[0] += 1
                ins.then_inc(dve_chain, 1)
                dve.wait_ge(dve_chain, chain[0])

            def variance(ln, b):
                for t in range(QT):
                    link(nc.vector.bn_stats(stats[:, t, :], xs[:, QT * b + t, :]))
                    link(nc.vector.bn_aggr(mv[:, ln, QT * b + t, :], stats[:, t, :]))
                nc.vector.tensor_scalar(veps[:, ln, QT * b:QT * b + QT], mv[:, ln, QT * b:QT * b + QT, 1],
                                        EPS, None, ALU.add).then_inc(var_ok, 1)

            def normalise(b):
                dve.wait_ge(rstd_ok, b + 1)
                if b:
                    dve.wait_ge(hT_ps, b)
                for t in range(QT):
                    i = QT * b + t
                    last = nc.vector.tensor_scalar(h1n[:, t, :], xs[:, i, :], mv[:, 0, i, 0:1], rstd[:, 0, i:i + 1],
                                                   ALU.subtract, ALU.mult)
                last.then_inc(h1n_ok, 1)

            def project(b):
                dve.wait_ge(hT_ok, KC * (b + 1))
                if b:
                    dve.wait_ge(v_ps, b)
                link(nc.vector.tensor_copy(hhi[:], hT[:]))
                nc.vector.tensor_tensor(hlo[:], hT[:], hhi[:].bitcast(F32), ALU.subtract).then_inc(h_ok, 1)
                for i, (hi, lo) in enumerate(((qhi_ok, qlo_ok), (khi_ok, klo_ok))):
                    dve.wait_ge(hi, b + 1)
                    for m in range(KC):
                        last = nc.vector.scalar_tensor_tensor(
                            out=qk[:, 2 * i + 1, m, :], in0=ps_qk[i][:, m, :], scalar=bqk[:, i, m:m + 1],
                            in1=qk[:, 2 * i, m, :].bitcast(F32), op0=ALU.add, op1=ALU.subtract)
                    last.then_inc(lo, 1)
                dve.wait_ge(v_ps, b + 1)
                if b == 0:
                    dve.wait_ge(ones_ok, 1)
                if b >= 3:
                    dve.wait_ge(pv_ps, 4 * (b - 2))
                for t in range(QT):
                    last = nc.vector.tensor_tensor(
                        va[:, b % 3, t, :, 0:DH], ps_v[:, t, :].rearrange("p (h d) -> p h d", h=HEADS),
                        bv_b[:].rearrange("p (h d) -> p h d", h=HEADS), ALU.add)
                last.then_inc(va_ok, 1)

            def row_max(b, u):
                hp, qt, gg = u % 2, u // 8, u // 2 % 4
                dve.wait_ge(s_ps, 16 * b + u + 1)
                nc.vector.reduce_max(mx[:, b % 2, qt, NG * hp + 2 * gg:NG * hp + 2 * gg + 2], ps_s[hp][:],
                                     AX.X).then_inc(mx_ok, 1)

            def maxima(b):
                dve.wait_ge(mhi_ok, b + 1)
                nc.vector.scalar_tensor_tensor(out=mneg[:, 1, :], in0=ps_w[0:HEADS, 0:L], scalar=-1.0,
                                               in1=mneg[:, 0, :].bitcast(F32), op0=ALU.mult,
                                               op1=ALU.subtract).then_inc(mlo_ok, 1)

            def divide(b, qt):
                o = ps_w[:].rearrange("p (h c) -> p h c", h=HEADS)
                dve.wait_ge(tr1_ps, QT * b + qt + 1)
                link(nc.vector.reciprocal(rden[:], o[:, :, DH]))
                nc.vector.tensor_tensor(on[:, qt, :].rearrange("p (h d) -> p h d", h=HEADS), o[:, :, 0:DH],
                                        rden[:].unsqueeze(2).broadcast_to([P, HEADS, DH]),
                                        ALU.mult).then_inc(on_ok, 1)

            def split_o(b):
                dve.wait_ge(ohi_ok, b + 1)
                nc.vector.tensor_tensor(olo[:], ps_wk, ohi[:].bitcast(F32), ALU.subtract).then_inc(olo_ok, 1)

            def residual(b):
                dve.wait_ge(wo_ps, b + 1)
                dve.wait_ge(xb_ok, b + 1)
                ga = gates[:, GA, b, :].unsqueeze(1).broadcast_to([P, QT, D])
                link(nc.vector.tensor_tensor(on[:], ps_wk, ga, ALU.mult))
                s = xs[:, QT * b:QT * b + QT, :]
                nc.vector.tensor_tensor(s, on[:], s, ALU.add).then_inc(x2_ok, 1)
                dve.wait_ge(x2_ok, b + 1)
                variance(1, b)

            def normalise2(b):
                dve.wait_ge(rstd_ok, B + b + 1)
                if b:
                    dve.wait_ge(h2_out, 16 * b)
                    dve.wait_ge(h2T_ps, b)
                for t in range(QT):
                    i = QT * b + t
                    last = nc.vector.tensor_scalar(h2r[:, t, :], xs[:, i, :], mv[:, 1, i, 0:1], rstd[:, 1, i:i + 1],
                                                   ALU.subtract, ALU.mult)
                last.then_inc(h2n_ok, 1)

            def choose(b):
                dve.wait_ge(lg_ps, b + 1)
                last = nc.vector.tensor_copy(lg[:], ps_w[:, 0:QT * NE].rearrange("p (t e) -> p t e", t=QT))
                last.then_inc(lg_ok, 1)
                dve.wait_ge(lg_ok, b + 1)
                for t in range(QT):
                    link(nc.vector.max(m8[:, t, :], lg[:, t, :]))
                    link(nc.vector.max_index(i8[:, t, :], m8[:, t, :], lg[:, t, :]))
                nc.vector.tensor_tensor(dlt[:], m8[:, :, 1], m8[:, :, 0], ALU.subtract).then_inc(dlt_ok, 1)
                link(nc.vector.tensor_copy(e12[:], i8[:, :, 0:2]))
                for t in range(QT):
                    last = nc.vector.tensor_tensor(hot[:, t], iota8[:].unsqueeze(1).broadcast_to([P, 2, NE]),
                                                   e12[:, t, :].unsqueeze(2).broadcast_to([P, 2, NE]), ALU.is_equal)
                    link(last)
                nc.vector.tensor_tensor(picked[:, QT * b:QT * b + QT, :], hot[:, :, 0, :], hot[:, :, 1, :],
                                        ALU.add).then_inc(picked_ok, 1)

            def weigh(b):
                dve.wait_ge(edlt_ok, b + 1)
                if b:
                    dve.wait_ge(routed, 64 * b)
                nc.vector.tensor_copy(info[:, :, TOK], token[:, QT * b:QT * b + QT])
                nc.vector.tensor_copy(info[:, :, E1], e12[:, :, 0])
                link(nc.vector.tensor_scalar(wsum[:], edlt[:], 1.0, None, ALU.add))
                link(nc.vector.reciprocal(wsum[:], wsum[:]))
                link(nc.vector.tensor_tensor(info[:, :, W2], edlt[:], wsum[:], ALU.mult))
                link(nc.vector.tensor_tensor(info[:, :, DW], wsum[:], info[:, :, W2], ALU.subtract))

            def place(b):
                dve.wait_ge(rank_ps, b + 1)
                nc.vector.tensor_tensor(pos[:], ps_w[:, 0:QT * NE].rearrange("p (t e) -> p t e", t=QT),
                                        region[:].unsqueeze(1).broadcast_to([P, QT, NE]), ALU.add).then_inc(pos_ok, 1)
                dve.wait_ge(pos_ok, b + 1)
                for t in range(QT):
                    link(nc.vector.tensor_tensor(hot[:, t], hot[:, t], pos[:, t, :].unsqueeze(1).broadcast_to([P, 2, NE]),
                                                 ALU.mult))
                link(nc.vector.tensor_reduce(slotf[:], hot[:], AX.X, ALU.add))
                nc.vector.tensor_copy(slot[:], slotf[:]).then_inc(slot_ok, 1)

            def plan():
                def per_tile(t):
                    return t[:].unsqueeze(2).broadcast_to([P, NT, NE])

                def per_expert(t, n=NT):
                    return t[:].unsqueeze(1).broadcast_to([P, n, NE])

                dve.wait_ge(count_ps, 1)
                link(nc.vector.tensor_copy(count[:], ps_w[:, 0:NE]))
                link(nc.vector.tensor_tensor(prod[:, 0:NE, :], count[:].unsqueeze(2).broadcast_to([P, NE, NE]),
                                             per_expert(steps, NE), ALU.is_gt))
                link(nc.vector.tensor_reduce(tiles[:], prod[:, 0:NE, :], AX.X, ALU.add))
                link(nc.vector.tensor_tensor_scan(tend[:], ones8[:], tiles[:], 0.0, ALU.mult, ALU.add))
                link(nc.vector.tensor_tensor(tbeg[:], tend[:], tiles[:], ALU.subtract))
                link(nc.vector.tensor_tensor(prod[:], per_expert(tend), per_tile(tile_no), ALU.is_le))
                link(nc.vector.tensor_reduce(texp[:], prod[:], AX.X, ALU.add))
                link(nc.vector.tensor_scalar(texp[:], texp[:], NE - 1.0, None, ALU.min))
                link(nc.vector.tensor_copy(texp_i[:], texp[:]))
                link(nc.vector.tensor_tensor(pick[:], per_expert(iota8), per_tile(texp), ALU.is_equal))
                link(nc.vector.tensor_tensor(prod[:], pick[:], per_expert(tbeg), ALU.mult))
                link(nc.vector.tensor_reduce(tbase[:], prod[:], AX.X, ALU.add))
                link(nc.vector.tensor_tensor(prod[:], pick[:], per_expert(count), ALU.mult))
                link(nc.vector.tensor_reduce(tcount[:], prod[:], AX.X, ALU.add))
                link(nc.vector.scalar_tensor_tensor(out=trow[:], in0=tbase[:], scalar=-float(P), in1=tile_row[:],
                                                    op0=ALU.mult, op1=ALU.add))
                link(nc.vector.tensor_tensor(valid[:], trow[:], tcount[:], ALU.is_lt))
                link(nc.vector.scalar_tensor_tensor(out=trow[:], in0=texp[:], scalar=float(B * L), in1=trow[:],
                                                    op0=ALU.mult, op1=ALU.add))
                link(nc.vector.scalar_tensor_tensor(out=trow[:], in0=trow[:], scalar=pad_row[:], in1=valid[:],
                                                    op0=ALU.subtract, op1=ALU.mult))
                nc.vector.tensor_scalar(gidx[:], trow[:], pad_row[:], None, ALU.add).then_inc(plan_ok, 1)

            dve.wait_ge(x_in[0], 16)
            variance(0, 0)
            dve.wait_ge(mod_ps, 1)
            for n in range(3):
                last = nc.vector.tensor_copy(mrow[32 * n:32 * n + B, :],
                                             ps_s[0][32 * n:32 * n + B].rearrange("p a b -> p (a b)"))
                if n == 0:
                    last.then_inc(mrow_ok, 1)
            link(last)
            cb = mrow[64:64 + B, 0:D]
            nc.vector.tensor_scalar(cb, cb, 1.0, None, ALU.add)
            for r, c in ((32, 0), (64, D)):
                g, s, a = mrow[r:r + B, c:c + D], gsign[r:r + B, :], gabs[r:r + B, :]
                link(nc.vector.tensor_scalar(s, g, 0.0, 2.0, ALU.is_ge, ALU.mult))
                link(nc.vector.scalar_tensor_tensor(out=a, in0=s, scalar=-1.0, in1=g, op0=ALU.add, op1=ALU.mult))
                link(nc.vector.tensor_scalar(a, a, 0.25, None, ALU.max))
                nc.vector.scalar_tensor_tensor(out=g, in0=s, scalar=-1.0, in1=a, op0=ALU.add,
                                               op1=ALU.mult).then_inc(mrow_ok, 1)
            dve.wait_ge(modT_ps, 1)
            nc.vector.tensor_copy(modT[:, 0:2, :], ps_w[:, 0:2 * B].rearrange("p (j b) -> p j b", j=2))
            nc.vector.tensor_scalar(modT[:, 2:4, :], ps_w[:, 2 * B:4 * B].rearrange("p (j b) -> p j b", j=2),
                                    1.0, None, ALU.add).then_inc(modT_ok, 1)
            normalise(0)
            dve.wait_ge(wraw_in, 64)
            for s in (slice(0, 3), slice(3, 4)):
                link(nc.vector.tensor_copy(whi[:, s], w_raw[:, s]))
                nc.vector.tensor_tensor(wlo[:, s], w_raw[:, s], whi[:, s].bitcast(F32),
                                        ALU.subtract).then_inc(wsplit_ok, 1)
            project(0)
            for b in range(1, B):
                dve.wait_ge(x_in[b], 16)
                variance(0, b)
                if b == 1:
                    normalise(1)
                    project(1)
            for u in range(16):
                row_max(0, u)
            maxima(0)
            for b in range(B):
                if b + 2 < B:
                    normalise(b + 2)
                    project(b + 2)
                for u in range(16):
                    if b + 1 < B:
                        row_max(b + 1, u)
                    if b:
                        if u in (1, 3):
                            divide(b - 1, u // 2)
                        if u == 9:
                            split_o(b - 1)
                        if u == 12:
                            residual(b - 1)
                    if b >= 2:
                        if u == 10:
                            choose(b - 2)
                        if u == 13:
                            weigh(b - 2)
                        if u == 15:
                            place(b - 2)
                if b + 1 < B:
                    maxima(b + 1)
                if b:
                    normalise2(b - 1)
            choose(B - 2)
            weigh(B - 2)
            place(B - 2)
            for qt in range(QT):
                divide(B - 1, qt)
            split_o(B - 1)
            residual(B - 1)
            normalise2(B - 1)
            choose(B - 1)
            weigh(B - 1)
            place(B - 1)
            plan()

            def gate_up(i, par):
                j = 2 * i + par
                dve.wait_ge(act0_ok, j + 1)
                nc.vector.tensor_tensor(inter[par][:], ps_h[par][:, 1, :], act0[par][:], ALU.mult).then_inc(inter_ok, 1)

            def keep_i(i, par):
                j = 2 * i + par
                dve.wait_ge(i_ps, j + 1)
                nc.vector.tensor_copy(iT[par][:].rearrange("p m t -> p (m t)"), ps_i).then_inc(iT_ok, 1)

            dve.sem_inc(inter_ok, 2)
            dve.sem_inc(iT_ok, 1)
            gate_up(0, 0)
            with dve.Fori(0, (NT - 1) // 2) as i:
                for par in range(2):
                    keep_i(i, par)
                    gate_up(i + par, 1 - par)
            keep_i((NT - 1) // 2, 0)

            for b in range(B):
                a = acc[:, QT * b:QT * b + QT, :]
                dve.wait_ge(acc_in[b], 16)
                link(nc.vector.tensor_tensor(a, a, gates[:, GB, b, :].unsqueeze(1).broadcast_to([P, QT, D]), ALU.mult))
                nc.vector.tensor_tensor(a, a, xs[:, QT * b:QT * b + QT, :], ALU.add).then_inc(res_ok, 1)

        @block.tensor
        def _(pe):
            w_reader = [None]

            def take_w():
                if w_reader[0]:
                    pe.wait_ge(*w_reader[0])

            def three(out, stat, mov, first, last):
                for i, (s, m) in enumerate(((stat[0], mov[0]), (stat[0], mov[1]), (stat[1], mov[0]))):
                    ins = nc.tensor.matmul(out, s, m, start=first and i == 0, stop=last and i == 2)
                return ins

            def project(b):
                pe.wait_ge(h1n_ok, b + 1)
                take_w()
                for k in range(KC):
                    for t in range(QT):
                        last = nc.tensor.transpose(ps_wk[:, k, P * t:P * t + P], h1n[:, t, P * k:P * k + P], ident[:])
                last.then_inc(hT_ps, 1)
                w_reader[0] = (hT_ok, KC * (b + 1))
                pe.wait_ge(wsplit_ok, 1)
                pe.wait_ge(h_ok, b + 1)
                if b >= 3:
                    pe.wait_ge(exp_ok, NG * (b - 2))
                elif b >= 1:
                    pe.wait_ge(klo_ok, b)
                    pe.wait_ge(va_ok, b)
                for i, done in enumerate((q_ps, k_ps)):
                    for m in range(KC):
                        for k in range(KC):
                            c = slice(P * m, P * m + P)
                            last = three(ps_qk[i][:, m, :], (whi[:, i, k, c], wlo[:, i, k, c]),
                                         (hhi[:, k, :], hlo[:, k, :]), k == 0, k == KC - 1)
                    last.then_inc(done, 1)
                for t in range(QT):
                    for k in range(KC):
                        c = slice(P * t, P * t + P)
                        last = three(ps_v[:, t, :], (hhi[:, k, c], hlo[:, k, c]),
                                     (whi[:, 2, k, :], wlo[:, 2, k, :]), k == 0, k == KC - 1)
                last.then_inc(v_ps, 1)

            def score(b, u):
                p, hp, qt, gg = b % 2, u % 2, u // 8, u // 2 % 4
                if u == 0:
                    pe.wait_ge(stack_in[p], 12 * 16 * (b // 2 + 1))
                if 16 * b + u >= 2:
                    pe.wait_ge(mx_ok, 16 * b + u - 1)
                r = HR * hp
                for i in range(2):
                    g = 2 * gg + i
                    last = nc.tensor.matmul(ps_s[hp][:, i, :], qs[r:r + K_MAX, p, g, P * qt:P * qt + P],
                                            ks[r:r + K_MAX, p, g, :], start=True, stop=True)
                last.then_inc(s_ps, 1)

            def maxima(b):
                pe.wait_ge(mx_ok, 16 * (b + 1))
                take_w()
                for qt in range(QT):
                    last = nc.tensor.transpose(ps_w[0:HEADS, P * qt:P * qt + P], mx[:, b % 2, qt, :], ident[:])
                last.then_inc(mT_ps, 1)
                w_reader[0] = (mlo_ok, b + 1)

            def score_T(b, g):
                p, u = b % 2, NG * b + g
                if g == 0:
                    pe.wait_ge(m_in[p], landed(b))
                    done = min(b + 3, B)
                    pe.wait_ge(klo_ok, done)
                    pe.wait_ge(va_ok, done)
                if u >= 2:
                    pe.wait_ge(exp_ok, u - 1)
                for hp in range(2):
                    r = HR * hp
                    for kc in range(QT):
                        last = nc.tensor.matmul(ps_t[g % 2][:, hp, L * kc:L * kc + L],
                                                ks[r:r + K_SUB, p, g, P * kc:P * kc + P],
                                                qs[r:r + K_SUB, p, g, :], start=True, stop=True)
                last.then_inc(t_ps, 1)

            def weighted(b, n):
                pe.wait_ge(exp_ok, NG * b + 2 * n + 2)
                if n % 2 == 0 and 4 * b + n:
                    pe.wait_ge(oT_ok, 2 * b + n // 2)
                for kc in range(QT):
                    for h in range(4 * n, 4 * n + 4):
                        r = 32 * (h % 4)
                        last = nc.tensor.matmul(ps_pv[r:r + 32, n % 2, :], va[:, b % 3, kc, h, :],
                                                probs[:, h // 2 % 4, h % 2, L * kc:L * kc + L],
                                                start=kc == 0, stop=kc == QT - 1)
                last.then_inc(pv_ps, 1)

            def o_rows(b, qt):
                pe.wait_ge(oT_ok, 2 * (b + 1))
                take_w()
                for n in range(HEADS // 4):
                    last = nc.tensor.transpose(ps_w[:, P * n:P * n + P], oT[:, n, P * qt:P * qt + P], ident[:])
                last.then_inc(tr1_ps, 1)
                w_reader[0] = (on_ok, QT * b + qt + 1)

            def o_columns(b):
                pe.wait_ge(on_ok, QT * (b + 1))
                take_w()
                for k in range(KC):
                    for qt in range(QT):
                        last = nc.tensor.transpose(ps_wk[:, k, P * qt:P * qt + P], on[:, qt, P * k:P * k + P], ident[:])
                last.then_inc(tr2_ps, 1)
                w_reader[0] = (olo_ok, b + 1)

            def project_o(b):
                pe.wait_ge(olo_ok, b + 1)
                take_w()
                pe.wait_ge(wsplit_ok, 2)
                for qt in range(QT):
                    for k in range(KC):
                        c = slice(P * qt, P * qt + P)
                        last = three(ps_wk[:, qt, :], (ohi[:, k, c], olo[:, k, c]),
                                     (whi[:, 3, k, :], wlo[:, 3, k, :]), k == 0, k == KC - 1)
                last.then_inc(wo_ps, 1)
                w_reader[0] = (x2_ok, b + 1)

            def h2_columns(b):
                pe.wait_ge(h2_ok, b + 1)
                take_w()
                for k in range(KC):
                    for t in range(QT):
                        last = nc.tensor.transpose(ps_wk[:, k, P * t:P * t + P], h2r[:, t, P * k:P * k + P], ident[:])
                last.then_inc(h2T_ps, 1)
                w_reader[0] = (h2T_ok, b + 1)

            def logits(b):
                take_w()
                for t in range(QT):
                    for k in range(KC):
                        last = nc.tensor.matmul(ps_w[:, NE * t:NE * t + NE], h2T[:, k, P * t:P * t + P],
                                                gate_sb[:, k, :], start=k == 0, stop=k == KC - 1)
                last.then_inc(lg_ps, 1)
                w_reader[0] = (lg_ok, b + 1)

            def ranks(b):
                pe.wait_ge(picked_ok, b + 1)
                pe.wait_ge(const_ok, 1)
                take_w()
                for t in range(QT):
                    i = QT * b + t
                    for n in range(i + 1):
                        last = nc.tensor.matmul(ps_w[:, NE * t:NE * t + NE], upper[:] if n == i else ones_bf[:],
                                                picked[:, n, :], start=n == 0, stop=n == i)
                last.then_inc(rank_ps, 1)
                w_reader[0] = (pos_ok, b + 1)

            pe.wait_ge(silu_ok, 1)
            pe.wait_ge(wmod_in, 32)
            for k in range(KC):
                for n in range(3):
                    last = nc.tensor.matmul(ps_s[0][32 * n:32 * n + B].rearrange("p a b -> p (a b)"), sc[:, k, :],
                                            wmod_sb[:, k, 2 * D * n:2 * D * n + 2 * D], start=k == 0, stop=k == KC - 1)
            last.then_inc(mod_ps, 1)
            pe.wait_ge(mrow_ok, 1)
            pe.wait_ge(ident_ok, 1)
            for j in range(4):
                last = nc.tensor.transpose(ps_w[:, B * j:B * j + B], mrow[0:B, P * j:P * j + P], ident[0:B, 0:B])
            last.then_inc(modT_ps, 1)
            w_reader[0] = (modT_ok, 1)

            project(0)
            project(1)
            for u in range(16):
                score(0, u)
            maxima(0)
            for b in range(B):
                if b + 2 < B:
                    project(b + 2)
                for g in range(NG):
                    score_T(b, g)
                    if b + 1 < B:
                        score(b + 1, 2 * g)
                        score(b + 1, 2 * g + 1)
                    if g in (2, 4, 6):
                        weighted(b, g // 2 - 1)
                    if b:
                        if g < QT:
                            o_rows(b - 1, g)
                        elif g == 3:
                            o_columns(b - 1)
                        elif g == 5:
                            project_o(b - 1)
                    if b >= 2:
                        if g == 2:
                            h2_columns(b - 2)
                        elif g == 4:
                            logits(b - 2)
                        elif g == 6:
                            ranks(b - 2)
                weighted(b, 3)
                if b + 1 < B:
                    maxima(b + 1)
            h2_columns(B - 2)
            logits(B - 2)
            ranks(B - 2)
            for qt in range(QT):
                o_rows(B - 1, qt)
            o_columns(B - 1)
            project_o(B - 1)
            h2_columns(B - 1)
            logits(B - 1)
            ranks(B - 1)
            take_w()
            for n in range(T):
                last = nc.tensor.matmul(ps_w[:, 0:NE], ones_bf[:], picked[:, n, :], start=n == 0, stop=n == T - 1)
            last.then_inc(count_ps, 1)

            def columns_x(i, par):
                j = 2 * i + par
                pe.wait_ge(xg_in[par], 16 * i + 16)
                pe.wait_ge(xT_ok, j)
                for k in range(KC):
                    last = nc.tensor.transpose(ps_x[:, k, :], xg[par][:, P * k:P * k + P], ident[:])
                last.then_inc(x_ps, 1)

            def expert(i, par):
                return pe.value_load(texp_i[0:1, bass.ds(2 * i + par, 1)], min_val=0, max_val=NE - 1)

            def hidden(i, par):
                j = 2 * i + par
                e = expert(i, par)
                pe.wait_ge(xT_ok, j + 1)
                pe.wait_ge(inter_ok, j + 1)
                for n in range(2):
                    for k in range(KC):
                        last = nc.tensor.matmul(ps_h[par][:, n, :], xT[par][:, k, :],
                                                w01[:, bass.ds(e, 1), k, F * n:F * n + F],
                                                start=k == 0, stop=k == KC - 1)
                last.then_inc(hid_ps, 1)

            def columns_i(i, par):
                j = 2 * i + par
                pe.wait_ge(inter_ok, j + 3)
                pe.wait_ge(iT_ok, j + 1)
                for m in range(FC):
                    last = nc.tensor.transpose(ps_i[:, P * m:P * m + P], inter[par][:, P * m:P * m + P], ident[:])
                last.then_inc(i_ps, 1)

            def down(i, par):
                j = 2 * i + par
                e = expert(i, par)
                pe.wait_ge(iT_ok, j + 2)
                pe.wait_ge(ys_ok, j + 1)
                for m in range(FC):
                    last = nc.tensor.matmul(ps_y[par], iT[par][:, m, :], wex[:, bass.ds(e, 1), m, :],
                                            start=m == 0, stop=m == FC - 1)
                last.then_inc(y_ps, 1)

            pe.wait_ge(plan_ok, 1)
            pe.wait_ge(oT_ok, 2 * B)
            columns_x(0, 0)
            columns_x(0, 1)
            pe.wait_ge(w01_in, 16 * 2 * NE)
            hidden(0, 0)
            pe.wait_ge(wex_in, 16 * NE)
            with pe.Fori(0, (NT - 3) // 2) as i:
                for par in range(2):
                    columns_i(i, par)
                    hidden(i + par, 1 - par)
                    down(i, par)
                    columns_x(i + 1, par)
            n = (NT - 3) // 2
            columns_i(n, 0)
            hidden(n, 1)
            down(n, 0)
            columns_x(n + 1, 0)
            columns_i(n, 1)
            hidden(n + 1, 0)
            down(n, 1)
            columns_i(n + 1, 0)
            down(n + 1, 0)


def kernel(**inputs):
    import numpy as np
    import concourse.bacc as bacc
    from concourse.bass_utils import run_bass_kernel_spmd

    nc = bacc.Bacc("TRN2", target_bir_lowering=False, num_devices=1)
    given = {n: np.asarray(a) for n, a in inputs.items()}
    names = ["L0_attn_x", "L0_attn_Wq", "L0_attn_bq", "L0_attn_Wk", "L0_attn_bk", "L0_attn_Wv", "L0_attn_bv",
             "L0_attn_Wo", "L0_attn_bo", "L0_ffn_gate_kernel", "L0_ffn_w0_kernel", "L0_ffn_w1_kernel",
             "L0_ffn_wo_kernel", "L0_c", "L0_wmod"]
    given["L0_c"] = given["L0_c"].T
    for n in ("L0_attn_bq", "L0_attn_bk"):
        given[n] = given[n].reshape(KC, P).T
    arrays, args = {}, []
    for n in names:
        a = np.ascontiguousarray(given[n])
        arrays[n] = a
        args.append(nc.dram_tensor(n, a.shape, mybir.dt.from_np(a.dtype), kind="ExternalInput").ap())
    out = nc.dram_tensor("out", (B, L, D), F32, kind="ExternalOutput").ap()
    adaln_block(nc, *args, out)
    r = run_bass_kernel_spmd(nc, [arrays], core_ids=[0])
    return r.results[0]["out"]
```

```python
from contextlib import ExitStack

import concourse.bass as bass
from concourse import mybir

F32 = mybir.dt.float32
F32R = mybir.dt.float32r
BF16 = mybir.dt.bfloat16
I32 = mybir.dt.int32
U32 = mybir.dt.uint32
ALU = mybir.AluOpType
ACT = mybir.ActivationFunctionType
AX = mybir.AxisListType

P = 128
B, L, D = 4, 256, 256
HEADS, DH = 16, 16
NE, F = 8, 512
KC = D // P
QT = L // P
T = B * QT
NG = HEADS // 2
HR = 64
K_MAX = 3 * DH
K_SUB = K_MAX + 2
FC = F // P
NT = (2 * B * L + NE * (P - 1)) // P
NB = NE * B * L // P + 1
TOK, E1, W2, DW = range(4)
EPS = 1e-5


def adaln_block(nc, x, wq, bq, wk, bk, wv, bv, wo, bo, gate, w0, w1, wout, cT, wmod, out):
    ctx = ExitStack()
    with ctx:
        top = [16512]

        def at(name, shape, dt, offset):
            return nc.alloc_sbuf_tensor_at(name, shape, dt, offset=offset)

        def sb(name, shape, dt):
            n = 4 if dt != BF16 else 2
            for s in shape[1:]:
                n *= s
            t = at(name, shape, dt, top[0])
            top[0] += (n + 31) // 32 * 32
            return t

        def sem(name):
            return ctx.enter_context(nc.semaphore(name))

        w01 = sb("w01", [P, NE, KC, 2 * F], F32)
        late = top[0]
        wex = sb("wex", [P, NE, FC, D], F32)
        probs = at("probs", [P, 4, 2, QT * L], F32, late)
        wmod_sb = at("wmod_sb", [P, KC, 6 * D], F32, late + 16384)
        h1n = at("h1n", [P, QT, D], F32, late + 28672)
        hT = at("hT", [P, KC, L], F32, late + 30720)
        xs = sb("xs", [P, T, D], F32)
        gates = sb("gates", [P, 4, B, D], F32)
        w_raw = at("w_raw", [P, 4, KC, D], F32, top[0] - 8192)
        GA, SBI, CB1, GB = range(4)
        bv_b = sb("bv_b", [P, D], F32)
        bo_b = sb("bo_b", [P, D], F32)
        gbo = sb("gbo", [P, D], F32)
        ident = sb("ident", [P, P], F32)
        bqk = sb("bqk", [P, 2, KC], F32)
        gate_sb = sb("gate_sb", [P, KC, NE], F32)
        cT_sb = sb("cT_sb", [P, KC, B], F32)
        sc = sb("sc", [P, KC, B], F32)
        modT = sb("modT", [P, 4, B], F32)
        mrow = sb("mrow", [P, 2 * D], F32)
        gsign = at("gsign", [P, D], F32, late + 16384)
        gabs = at("gabs", [P, D], F32, late + 17408)
        stats = sb("stats", [P, QT, 6], F32)
        mv = sb("mv", [P, 2, T, 2], F32)
        veps = sb("veps", [P, 2, T], F32)
        rstd = sb("rstd", [P, 2, T], F32)
        mhalf = sb("mhalf", [P, QT], F32)
        mx = sb("mx", [P, 2, QT, HEADS], F32)
        attn_top = top[0]
        whi = sb("whi", [P, 4, KC, D], F32R)
        wlo = sb("wlo", [P, 4, KC, D], F32R)
        qs = sb("qs", [P, 2, NG, L], F32R)
        ks = sb("ks", [P, 2, NG, L], F32R)
        va = sb("va", [P, 3, QT, HEADS, 32], F32)
        hhi = sb("hhi", [P, KC, L], F32R)
        hlo = sb("hlo", [P, KC, L], F32R)
        qk = sb("qk", [P, 4, KC, L], F32R)
        mneg = sb("mneg", [HEADS, 2, L], F32R)
        oT = at("oT", [P, HEADS // 4, L], F32, late + 16384)
        on = at("on", [P, QT, D], F32, late + 20480)
        ohi = at("ohi", [P, KC, L], F32R, late + 22528)
        olo = at("olo", [P, KC, L], F32R, late + 24576)
        rden = sb("rden", [P, HEADS], F32)
        h2r = sb("h2r", [P, QT, D], F32)
        info = sb("info", [P, QT, 4], F32)
        pad_info = sb("pad_info", [P, NB, 4], F32)
        h2T = sb("h2T", [P, KC, L], F32)
        iota8 = sb("iota8", [P, NE], F32)
        region = sb("region", [P, NE], F32)
        steps = sb("steps", [P, NE], F32)
        ones8 = sb("ones8", [P, NE], F32)
        tile_no = sb("tile_no", [P, NT], F32)
        block_expert = sb("block_expert", [P, NB], F32)
        token = sb("token", [P, T], F32)
        upper = sb("upper", [P, P], BF16)
        ones_bf = sb("ones_bf", [P, P], BF16)
        lg = sb("lg", [P, QT, NE], F32)
        m8 = sb("m8", [P, QT, 8], F32)
        i8 = sb("i8", [P, QT, 8], U32)
        dlt = sb("dlt", [P, QT], F32)
        edlt = sb("edlt", [P, QT], F32)
        wsum = sb("wsum", [P, QT], F32)
        e12 = sb("e12", [P, QT, 2], F32)
        hot = sb("hot", [P, QT, 2, NE], F32)
        picked = sb("picked", [P, T, NE], BF16)
        pos = sb("pos", [P, QT, NE], F32)
        slotf = sb("slotf", [P, QT, 2], F32)
        slot_n = sb("slot_n", [P, QT, 2], U32)
        slot_b = sb("slot_b", [P, QT, 2], U32)
        slot_p = sb("slot_p", [P, QT, 2], U32)
        slot = sb("slot", [P, QT, 2], U32)
        count = sb("count", [P, NE], F32)
        tiles = sb("tiles", [P, NE], F32)
        tend = sb("tend", [P, NE], F32)
        tbeg = sb("tbeg", [P, NE], F32)
        assert top[0] <= nc.sbuf_usable_end, top[0]
        top[0] = attn_top
        pick = sb("pick", [P, NT, NE], F32)
        prod = sb("prod", [P, NT, NE], F32)
        texp = sb("texp", [P, NT], F32)
        tbase = sb("tbase", [P, NT], F32)
        tblock = sb("tblock", [P, NT], F32)
        tblock_i = sb("tblock_i", [P, NT], I32)
        texp_i = sb("texp_i", [P, NT], I32)
        entries = sb("entries", [P, NB, 4], F32)
        tok = sb("tok", [P, NB], U32)
        wgt = sb("wgt", [P, NB], F32)
        tokg = [sb(f"tokg{i}", [P, 1], U32) for i in range(2)]
        toka = [sb(f"toka{i}", [P, 1], U32) for i in range(2)]
        xg = [sb(f"xg{i}", [P, D], F32) for i in range(2)]
        xT = [sb(f"xT{i}", [P, KC, P], F32) for i in range(2)]
        act0 = [sb(f"act0{i}", [P, F], F32) for i in range(2)]
        inter = [sb(f"inter{i}", [P, F], F32) for i in range(2)]
        iT = [sb(f"iT{i}", [P, FC, P], F32) for i in range(2)]
        ys = [sb(f"ys{i}", [P, D], F32) for i in range(2)]
        acc = sb("acc", [P, T, D], F32)
        assert top[0] <= nc.sbuf_usable_end, top[0]

        ps_s = [ctx.enter_context(nc.psum_tensor(f"ps_s{i}", [P, 2, L], F32)) for i in range(2)]
        ps_t = [ctx.enter_context(nc.psum_tensor(f"ps_t{i}", [P, 2, QT * L], F32)) for i in range(2)]
        ps_pv = ctx.enter_context(nc.psum_tensor("ps_pv", [P, 2, L], F32))
        ps_w = ctx.enter_context(nc.psum_tensor("ps_w", [P, 512], F32))
        ps_qk = [ps_t[0][:, i, :].rearrange("p (m t) -> p m t", m=KC) for i in range(2)]
        ps_v = ps_t[1][:, 0, :].rearrange("p (t n) -> p t n", t=QT)
        ps_wk = ps_w[:].rearrange("p (k t) -> p k t", k=2)
        ps_h = ps_t
        ps_x = ps_w[:, 0:KC * P].rearrange("p (k t) -> p k t", k=KC)
        ps_i = ps_pv[:].rearrange("p a b -> p (a b)")
        ps_y = [ps_s[i][:, 0, :] for i in range(2)]

        info_d = nc.dram_tensor("routed", (P * NB, 4), F32, kind="Internal").ap()
        h2_d = nc.dram_tensor("h2_rows", (B * L + P, D), F32, kind="Internal").ap()
        acc_d = nc.dram_tensor("mixture_sums", (B * L + P, D), F32, kind="Internal").ap()
        scratch = nc.dram_tensor("qk_scratch", (B, 4, D, L), F32, kind="Internal").ap()
        mod_d = nc.dram_tensor("mod_scratch", (4, B, D), F32, kind="Internal").ap()

        x_in = [sem(f"x_in{b}") for b in range(B)]
        c_in = sem("c_in")
        wmod_in = [sem(f"wmod_in{i}") for i in range(2)]
        wraw_in = [sem(f"wraw_in{i}") for i in range(2)]
        whi_ok = sem("whi_ok")
        small_in = sem("small_in")
        ident_ok = sem("ident_ok")
        zero_ok = sem("zero_ok")
        ones_ok = sem("ones_ok")
        dve_chain = sem("dve_chain")
        pool_chain = sem("pool_chain")
        silu_ok = sem("silu_ok")
        mod_ps = sem("mod_ps")
        mrow_ok = sem("mrow_ok")
        mrow23_ok = sem("mrow23_ok")
        gate_rows = sem("gate_rows")
        modT_ps = sem("modT_ps")
        modT_ok = sem("modT_ok")
        mod_out = sem("mod_out")
        gates_in = sem("gates_in")
        wsplit_ok = sem("wsplit_ok")
        var_ok = sem("var_ok")
        rstd_ok = sem("rstd_ok")
        h1n_ok = sem("h1n_ok")
        hT_ps = sem("hT_ps")
        hT_ok = sem("hT_ok")
        h_ok = sem("h_ok")
        q_ps = sem("q_ps")
        k_ps = sem("k_ps")
        v_ps = sem("v_ps")
        qhi_ok = sem("qhi_ok")
        khi_ok = sem("khi_ok")
        qlo_ok = sem("qlo_ok")
        klo_ok = sem("klo_ok")
        va_ok = sem("va_ok")
        qk_out = [sem(f"qk_out{p}") for p in range(2)]
        stack_in = [sem(f"stack_in{p}") for p in range(2)]
        s_ps = sem("s_ps")
        mx_ok = sem("mx_ok")
        mT_ps = sem("mT_ps")
        mhi_ok = sem("mhi_ok")
        mlo_ok = sem("mlo_ok")
        m_in = [sem(f"m_in{p}") for p in range(2)]
        t_ps = sem("t_ps")
        exp_ok = sem("exp_ok")
        pv_ps = sem("pv_ps")
        oT_ok = sem("oT_ok")
        tr1_ps = sem("tr1_ps")
        on_ok = sem("on_ok")
        tr2_ps = sem("tr2_ps")
        ohi_ok = sem("ohi_ok")
        olo_ok = sem("olo_ok")
        wo_ps = sem("wo_ps")
        xb_ok = sem("xb_ok")
        x2_ok = sem("x2_ok")
        w01_in = sem("w01_in")
        wex_in = sem("wex_in")
        pad_ok = sem("pad_ok")
        pad_out = sem("pad_out")
        const_ok = sem("const_ok")
        h2_ok = sem("h2_ok")
        h2T_ps = sem("h2T_ps")
        h2T_ok = sem("h2T_ok")
        lg_ps = sem("lg_ps")
        lg_ok = sem("lg_ok")
        dlt_ok = sem("dlt_ok")
        edlt_ok = sem("edlt_ok")
        picked_ok = sem("picked_ok")
        rank_ps = sem("rank_ps")
        slot_ok = sem("slot_ok")
        routed = sem("routed")
        count_ps = sem("count_ps")
        plan_ok = sem("plan_ok")
        xg_in = [sem(f"xg_in{i}") for i in range(2)]
        x_ps = sem("x_ps")
        xT_ok = sem("xT_ok")
        hid_ps = sem("hid_ps")
        act0_ok = sem("act0_ok")
        inter_ok = sem("inter_ok")
        i_ps = sem("i_ps")
        tokg_ok = sem("tokg_ok")
        toka_ok = sem("toka_ok")
        entries_in = sem("entries_in")
        h2_out = sem("h2_out")
        pool_waited = sem("pool_waited")
        tok_ok = sem("tok_ok")
        pos_ok = sem("pos_ok")
        iT_ok = sem("iT_ok")
        y_ps = sem("y_ps")
        wgt_ok = sem("wgt_ok")
        ys_ok = sem("ys_ok")
        y_added = [sem(f"y_added{i}") for i in range(2)]
        acc_in = [sem(f"acc_in{b}") for b in range(B)]
        res_ok = sem("res_ok")
        out_done = sem("out_done")

        def landed(b):
            return 64 * (b // 2 + 1)

        block = ctx.enter_context(nc.Block())

        @block.sync
        def _(sp):
            def rows(w):
                return w.rearrange("(k p) n -> p k n", p=P)

            def load_x(b):
                sp.dma_start(xs[:, QT * b:QT * b + QT, :],
                             x[b].rearrange("(t p) d -> p t d", p=P)).then_inc(x_in[b], 16)

            def load_w(i, w):
                sp.dma_start(w_raw[:, i], rows(w)).then_inc(wraw_in[i // 3], 16)

            sp.dma_start(cT_sb[:], rows(cT)).then_inc(c_in, 16)
            load_x(0)
            sp.dma_start(wmod_sb[:, :, 0:2 * D], rows(wmod)[:, :, 0:2 * D]).then_inc(wmod_in[0], 16)
            for i, w in enumerate((wq, wk, wv)):
                load_w(i, w)
            load_x(1)
            sp.dma_start(bqk[:, 0, :], bq).then_inc(small_in, 16)
            sp.dma_start(bqk[:, 1, :], bk).then_inc(small_in, 16)
            sp.dma_start(bv_b[:], bv.partition_broadcast(P)).then_inc(small_in, 16)
            sp.dma_start(bo_b[:], bo.partition_broadcast(P)).then_inc(small_in, 16)
            sp.dma_start(gate_sb[:], rows(gate)).then_inc(small_in, 16)
            for k in range(KC):
                sp.dma_start(wmod_sb[:, k, 2 * D:6 * D], wmod[P * k:P * k + P, 2 * D:6 * D]).then_inc(wmod_in[1], 16)
            load_w(3, wo)
            load_x(2)
            load_x(3)

            def unload(b):
                for i, ready in enumerate((qhi_ok, qlo_ok, khi_ok, klo_ok)):
                    sp.wait_ge(ready, b + 1)
                    sp.dma_start(scratch[b, i].rearrange("(m p) t -> p m t", p=P),
                                 qk[:, i].bitcast(F32)).then_inc(qk_out[b % 2], 16)

            def stack(b):
                p = b % 2
                sp.wait_ge(qk_out[p], landed(b))
                if b >= 2:
                    sp.wait_ge(t_ps, NG * (b - 1))
                else:
                    sp.wait_ge(ones_ok, 2 + p)
                for hp in range(2):
                    for dst, first, row, n in ((qs, 0, 0, 1), (qs, 0, 1, 2), (ks, 2, 0, 2), (ks, 2, 2, 1)):
                        r = HR * hp + DH * row
                        src = scratch[b, first:first + n].rearrange("s (g h d) t -> h s d g t", g=NG, h=2)[hp]
                        for i in range(n):
                            sp.dma_start(dst[r + DH * i:r + DH * i + DH, p, :, :].bitcast(F32), src[i]
                                         ).then_inc(stack_in[p], 16)

            def maxima(b):
                p = b % 2
                sp.wait_ge(mhi_ok, b + 1)
                sp.wait_ge(mlo_ok, b + 1)
                for hp in range(2):
                    for i in range(2):
                        r = HR * hp + K_MAX + i
                        sp.dma_start(qs[r:r + 1, p, :, :].bitcast(F32),
                                     mneg[NG * hp:NG * hp + NG, i, :].bitcast(F32)).then_inc(m_in[p], 16)

            def experts(first, n):
                for e in range(first, first + n):
                    for i, w in enumerate((w0, w1)):
                        sp.dma_start(w01[:, e, :, F * i:F * i + F], rows(w[e])).then_inc(w01_in, 16)

            unload(0)
            stack(0)
            unload(1)
            stack(1)
            sp.wait_ge(pad_ok, 2)
            sp.dma_start(acc_d.rearrange("(t p) d -> p t d", p=P),
                         h2T[:, 0, :].unsqueeze(1).broadcast_to([P, T + 1, D])).then_inc(pad_out, 16)
            sp.dma_start(h2_d[B * L:B * L + P], h2T[:, 0, :]).then_inc(pad_out, 16)
            sp.dma_start(info_d.rearrange("(p r) c -> p r c", p=P), pad_info[:]).then_inc(pad_out, 16)

            sp.wait_ge(gate_rows, 2)
            for i, (r, c) in ((GA, (32, 0)), (SBI, (32, D)), (CB1, (64, 0)), (GB, (64, D))):
                sp.dma_start(mod_d[i], mrow[r:r + B, c:c + D]).then_inc(mod_out, 16)
            sp.wait_ge(mod_out, 64)
            sp.wait_ge(wsplit_ok, 2)
            for i in range(4):
                sp.dma_start(gates[:, i], mod_d[i].partition_broadcast(P)).then_inc(gates_in, 16)
            maxima(0)
            for b in range(B):
                if b + 2 < B:
                    unload(b + 2)
                experts(2 * b, 2)
                if b + 2 < B:
                    stack(b + 2)
                if b + 1 < B:
                    maxima(b + 1)
            sp.wait_ge(x2_ok, B)
            for e in range(NE):
                sp.dma_start(wex[:, e], wout[e].rearrange("(m p) d -> p m d", p=P)).then_inc(wex_in, 16)
            sp.wait_ge(y_added[0], 16 * ((NT + 1) // 2))
            sp.wait_ge(y_added[1], 16 * (NT // 2))
            for b in range(B):
                sp.dma_start(acc[:, QT * b:QT * b + QT, :],
                             acc_d[L * b:L * b + L].rearrange("(t p) d -> p t d", p=P)).then_inc(acc_in[b], 16)
            for b in range(B):
                sp.wait_ge(res_ok, b + 1)
                sp.dma_start(out[b].rearrange("(t p) d -> p t d", p=P),
                             acc[:, QT * b:QT * b + QT, :]).then_inc(out_done, 16)
            sp.wait_ge(out_done, 16 * B)

        @block.gpsimd
        def _(pool):
            chain = [0]

            def link(ins):
                chain[0] += 1
                ins.then_inc(pool_chain, 1)
                pool.wait_ge(pool_chain, chain[0])

            link(nc.gpsimd.memset(ident[:], 0.0))
            nc.gpsimd.affine_select(out=ident[:], in_=ident[:], compare_op=ALU.not_equal, fill=1.0, base=0,
                                    pattern=[[-1, P]], channel_multiplier=1).then_inc(ident_ok, 1)
            def rsqrt(ln, b):
                pool.wait_ge(var_ok, B * ln + b + 1)
                s = slice(QT * b, QT * b + QT)
                nc.gpsimd.tensor_tensor(rstd[:, ln, s], veps[:, ln, s], mhalf[:], ALU.pow).then_inc(rstd_ok, 1)

            link(nc.gpsimd.memset(mhalf[:], -0.5))
            rsqrt(0, 0)
            nc.gpsimd.memset(va[:], 1.0).then_inc(ones_ok, 1)
            rsqrt(0, 1)
            for p in range(2):
                nc.gpsimd.memset(ks[:, p].bitcast(F32), 1.0).then_inc(ones_ok, 1)

            for t, pattern, base, mult in ((iota8[:], [[1, NE]], 0, 0), (region[:], [[B * L, NE]], 0, 0),
                                           (steps[:], [[P, NE]], 0, 0), (tile_no[:], [[1, NT]], 0, 0),
                                           (token[:], [[P, T]], 0, 1),
                                           (block_expert[:, 0:NB - 1], [[1, NE], [0, T]], 0, 0)):
                nc.gpsimd.iota(t, pattern, base=base, channel_multiplier=mult, allow_small_or_imprecise_dtypes=True)
            link(nc.gpsimd.memset(upper[:], 1.0))
            nc.gpsimd.affine_select(out=upper[:], in_=upper[:], compare_op=ALU.is_gt, fill=0.0, base=0,
                                    pattern=[[1, P]], channel_multiplier=-1)
            nc.gpsimd.memset(block_expert[:, NB - 1:NB], -1.0)
            nc.gpsimd.memset(ones8[:], 1.0)
            nc.gpsimd.memset(ones_bf[:], 1.0).then_inc(const_ok, 1)
            link(nc.gpsimd.memset(pad_info[:], 0.0))
            nc.gpsimd.iota(pad_info[:, :, TOK], [[0, NB]], base=B * L, channel_multiplier=1,
                           allow_small_or_imprecise_dtypes=True).then_inc(pad_ok, 1)
            nc.gpsimd.memset(h2T[:], 0.0).then_inc(pad_ok, 1)

            for b in range(2, B):
                rsqrt(0, b)
            pool.wait_ge(gates_in, 64)
            pool.wait_ge(small_in, 80)
            for b in range(B):
                link(nc.gpsimd.tensor_tensor(gbo[:], bo_b[:], gates[:, GA, b, :], ALU.mult))
                pool.wait_ge(h1n_ok, b + 1)
                for t in range(QT):
                    last = nc.gpsimd.tensor_tensor(xs[:, QT * b + t, :], xs[:, QT * b + t, :], gbo[:], ALU.add)
                    link(last)
                pool.sem_inc(xb_ok, 1)

            def keep_h2(b):
                pool.wait_ge(h2_ok, b + 1)
                pool.dma_start(h2_d[L * b:L * b + L].rearrange("(t p) d -> p t d", p=P), h2r[:]).then_inc(h2_out, 16)

            def route(b):
                pool.wait_ge(slot_ok, b + 1)
                if b == 0:
                    pool.wait_ge(pad_out, 48)
                for t in range(QT):
                    for c in range(2):
                        nc.gpsimd.indirect_dma_start(
                            out=info_d, out_offset=bass.IndirectOffsetOnAxis(ap=slot[:, t, c:c + 1], axis=0),
                            in_=info[:, t, :], in_offset=None).then_inc(routed, 16)

            for b in range(B):
                rsqrt(1, b)
                keep_h2(b)
                route(b)

            def apart():
                pool.sem_inc(pool_waited, 1)

            def gather(i, par, wait=True):
                j = 2 * i + par
                blk = pool.value_load(tblock_i[0:1, bass.ds(j, 1)], min_val=0, max_val=NB - 1)
                if wait:
                    pool.wait_ge(x_ps, j - 1)
                    apart()
                nc.gpsimd.tensor_copy(tokg[par][:], tok[:, bass.ds(blk, 1)]).then_inc(tokg_ok, 1)
                pool.wait_ge(tokg_ok, j + 1)
                apart()
                nc.gpsimd.indirect_dma_start(
                    out=xg[par][:], out_offset=None, in_=h2_d,
                    in_offset=bass.IndirectOffsetOnAxis(ap=tokg[par][:], axis=0)).then_inc(xg_in[par], 16)

            def add_rows(i, par):
                j = 2 * i + par
                blk = pool.value_load(tblock_i[0:1, bass.ds(j, 1)], min_val=0, max_val=NB - 1)
                if not isinstance(i, int) or i + par:
                    pool.wait_ge(y_added[1 - par], 16 * i + 16 * par)
                    apart()
                nc.gpsimd.tensor_copy(toka[par][:], tok[:, bass.ds(blk, 1)]).then_inc(toka_ok, 1)
                pool.wait_ge(toka_ok, j + 1)
                pool.wait_ge(ys_ok, j + 3)
                apart()
                nc.gpsimd.indirect_dma_start(
                    out=acc_d, out_offset=bass.IndirectOffsetOnAxis(ap=toka[par][:], axis=0),
                    in_=ys[par][:], in_offset=None, compute_op=ALU.add).then_inc(y_added[par], 16)

            pool.wait_ge(routed, 64 * B)
            pool.wait_ge(wo_ps, B)
            pool.dma_start(entries[:], info_d.rearrange("(p r) c -> p r c", p=P)).then_inc(entries_in, 16)
            pool.wait_ge(h2_out, 16 * B)
            pool.wait_ge(plan_ok, 1)
            pool.wait_ge(tok_ok, 1)
            gather(0, 0, wait=False)
            gather(0, 1, wait=False)
            gather(1, 0)
            n = (NT - 3) // 2

            def two_tiles(i):
                gather(i + 1, 1)
                add_rows(i, 0)
                gather(i + 2, 0)
                add_rows(i, 1)

            two_tiles(0)
            with pool.Fori(1, n - 1) as i:
                two_tiles(i)
            gather(n, 1)
            add_rows(n - 1, 0)
            gather(n + 1, 0)
            add_rows(n - 1, 1)
            for j in range(2 * n, NT):
                add_rows(j // 2, j % 2)

        @block.scalar
        def _(act):
            act.wait_ge(c_in, 16)
            nc.scalar.activation(sc[:], cT_sb[:], ACT.Silu).then_inc(silu_ok, 1)

            def modulate(b):
                act.wait_ge(hT_ps, b + 1)
                act.wait_ge(modT_ok, 1)
                if b:
                    act.wait_ge(h_ok, b)
                for k in range(KC):
                    nc.scalar.activation(hT[:, k, :], ps_wk[:, k, :], ACT.Identity, scale=modT[:, 2 + k, b:b + 1],
                                         bias=modT[:, k, b:b + 1]).then_inc(hT_ok, 1)

            def keep_qk(b):
                act.wait_ge(small_in, 80)
                for i, (done, ready) in enumerate(((q_ps, qhi_ok), (k_ps, khi_ok))):
                    act.wait_ge(done, b + 1)
                    if b:
                        act.wait_ge(qk_out[(b - 1) % 2], landed(b - 1))
                    for m in range(KC):
                        last = nc.scalar.activation(qk[:, 2 * i, m, :], ps_qk[i][:, m, :], ACT.Identity,
                                                    bias=bqk[:, i, m:m + 1])
                    last.then_inc(ready, 1)

            def maxima(b):
                act.wait_ge(mT_ps, b + 1)
                if b:
                    act.wait_ge(m_in[(b - 1) % 2], landed(b - 1))
                nc.scalar.activation(mneg[:, 0, :], ps_w[0:HEADS, 0:L], ACT.Copy, scale=-1.0).then_inc(mhi_ok, 1)

            def exponentials(b, g):
                u = NG * b + g
                act.wait_ge(t_ps, u + 1)
                if u >= 4:
                    act.wait_ge(pv_ps, u // 2 - 1)
                nc.scalar.activation(probs[:, g % 4], ps_t[g % 2][:], ACT.Exp, scale=1.0 / DH).then_inc(exp_ok, 1)

            def keep_o(b, half):
                act.wait_ge(pv_ps, 4 * b + 2 * half + 2)
                if b:
                    act.wait_ge(tr1_ps, QT * b)
                nc.scalar.activation(oT[:, 2 * half:2 * half + 2, :], ps_pv[:], ACT.Copy).then_inc(oT_ok, 1)

            def split_o(b):
                act.wait_ge(tr2_ps, b + 1)
                if b:
                    act.wait_ge(wo_ps, b)
                nc.scalar.activation(ohi[:], ps_wk, ACT.Copy).then_inc(ohi_ok, 1)

            def keep_h2T(b):
                act.wait_ge(h2T_ps, b + 1)
                if b:
                    act.wait_ge(lg_ps, b)
                else:
                    act.wait_ge(pad_out, 48)
                nc.scalar.activation(h2T[:], ps_wk, ACT.Copy).then_inc(h2T_ok, 1)

            def exp_gap(b):
                act.wait_ge(dlt_ok, b + 1)
                nc.scalar.activation(edlt[:], dlt[:], ACT.Exp).then_inc(edlt_ok, 1)

            act.wait_ge(wraw_in[0], 48)
            nc.scalar.activation(whi[:, 0:3], w_raw[:, 0:3], ACT.Copy).then_inc(whi_ok, 1)
            modulate(0)
            modulate(1)
            keep_qk(0)
            act.wait_ge(mod_ps, 2)
            for n in (1, 2):
                nc.scalar.activation(mrow[32 * n:32 * n + B, :], ps_s[0][32 * n:32 * n + B].rearrange("p a b -> p (a b)"),
                                     ACT.Copy).then_inc(mrow23_ok, 1)
            act.wait_ge(wraw_in[1], 16)
            nc.scalar.activation(whi[:, 3], w_raw[:, 3], ACT.Copy).then_inc(whi_ok, 1)
            keep_qk(1)
            maxima(0)
            for b in range(B):
                if b + 2 < B:
                    modulate(b + 2)
                    keep_qk(b + 2)
                for g in range(NG):
                    exponentials(b, g)
                    if b:
                        if g == 2:
                            split_o(b - 1)
                        elif g == 5:
                            keep_h2T(b - 1)
                        elif g == 7:
                            exp_gap(b - 1)
                    if g == 5:
                        keep_o(b, 0)
                if b + 1 < B:
                    maxima(b + 1)
                keep_o(b, 1)
            split_o(B - 1)
            keep_h2T(B - 1)
            exp_gap(B - 1)

            def keep_x(i, par):
                j = 2 * i + par
                act.wait_ge(x_ps, j + 1)
                nc.scalar.activation(xT[par][:], ps_x, ACT.Copy).then_inc(xT_ok, 1)

            def silu(i, par):
                j = 2 * i + par
                act.wait_ge(hid_ps, j + 1)
                act.wait_ge(inter_ok, j + 1)
                nc.scalar.activation(act0[par][:], ps_h[par][:, 0, :], ACT.Silu).then_inc(act0_ok, 1)

            def scale_y(i, par):
                j = 2 * i + par
                blk = act.value_load(tblock_i[0:1, bass.ds(j, 1)], min_val=0, max_val=NB - 1)
                act.wait_ge(y_ps, j + 1)
                if not isinstance(i, int) or i:
                    act.wait_ge(y_added[par], 16 * i)
                nc.scalar.activation(ys[par][:], ps_y[par], ACT.Copy, scale=wgt[:, bass.ds(blk, 1)]).then_inc(ys_ok, 1)

            act.sem_inc(ys_ok, 2)
            act.wait_ge(plan_ok, 1)
            act.wait_ge(wgt_ok, 1)
            keep_x(0, 0)
            keep_x(0, 1)
            silu(0, 0)
            n = (NT - 3) // 2

            def two_tiles(i):
                for par in range(2):
                    silu(i + par, 1 - par)
                    keep_x(i + 1, par)
                    scale_y(i, par)

            two_tiles(0)
            with act.Fori(1, n) as i:
                two_tiles(i)
            silu(n, 1)
            keep_x(n + 1, 0)
            scale_y(n, 0)
            silu(n + 1, 0)
            scale_y(n, 1)
            scale_y(n + 1, 0)

        @block.vector
        def _(dve):
            chain = [0]

            def link(ins):
                chain[0] += 1
                ins.then_inc(dve_chain, 1)
                dve.wait_ge(dve_chain, chain[0])

            def variance(ln, b):
                for t in range(QT):
                    link(nc.vector.bn_stats(stats[:, t, :], xs[:, QT * b + t, :]))
                    link(nc.vector.bn_aggr(mv[:, ln, QT * b + t, :], stats[:, t, :]))
                nc.vector.tensor_scalar(veps[:, ln, QT * b:QT * b + QT], mv[:, ln, QT * b:QT * b + QT, 1],
                                        EPS, None, ALU.add).then_inc(var_ok, 1)

            def normalise(b):
                dve.wait_ge(rstd_ok, b + 1)
                if b:
                    dve.wait_ge(hT_ps, b)
                for t in range(QT):
                    i = QT * b + t
                    last = nc.vector.tensor_scalar(h1n[:, t, :], xs[:, i, :], mv[:, 0, i, 0:1], rstd[:, 0, i:i + 1],
                                                   ALU.subtract, ALU.mult)
                last.then_inc(h1n_ok, 1)

            def split_h(b):
                dve.wait_ge(hT_ok, KC * (b + 1))
                if b:
                    dve.wait_ge(v_ps, b)
                link(nc.vector.tensor_copy(hhi[:], hT[:]))
                nc.vector.tensor_tensor(hlo[:], hT[:], hhi[:].bitcast(F32), ALU.subtract).then_inc(h_ok, 1)

            def keep_qkv(b):
                for i, (hi, lo) in enumerate(((qhi_ok, qlo_ok), (khi_ok, klo_ok))):
                    dve.wait_ge(hi, b + 1)
                    for m in range(KC):
                        last = nc.vector.scalar_tensor_tensor(
                            out=qk[:, 2 * i + 1, m, :], in0=ps_qk[i][:, m, :], scalar=bqk[:, i, m:m + 1],
                            in1=qk[:, 2 * i, m, :].bitcast(F32), op0=ALU.add, op1=ALU.subtract)
                    last.then_inc(lo, 1)
                dve.wait_ge(v_ps, b + 1)
                if b == 0:
                    dve.wait_ge(ones_ok, 1)
                if b >= 3:
                    dve.wait_ge(pv_ps, 4 * (b - 2))
                for t in range(QT):
                    last = nc.vector.tensor_tensor(
                        va[:, b % 3, t, :, 0:DH], ps_v[:, t, :].rearrange("p (h d) -> p h d", h=HEADS),
                        bv_b[:].rearrange("p (h d) -> p h d", h=HEADS), ALU.add)
                last.then_inc(va_ok, 1)

            def row_max(b, u):
                hp, qt, gg = u % 2, u // 8, u // 2 % 4
                dve.wait_ge(s_ps, 16 * b + u + 1)
                nc.vector.reduce_max(mx[:, b % 2, qt, NG * hp + 2 * gg:NG * hp + 2 * gg + 2], ps_s[hp][:],
                                     AX.X).then_inc(mx_ok, 1)

            def maxima(b):
                dve.wait_ge(mhi_ok, b + 1)
                nc.vector.scalar_tensor_tensor(out=mneg[:, 1, :], in0=ps_w[0:HEADS, 0:L], scalar=-1.0,
                                               in1=mneg[:, 0, :].bitcast(F32), op0=ALU.mult,
                                               op1=ALU.subtract).then_inc(mlo_ok, 1)

            def divide(b, qt):
                o = ps_w[:].rearrange("p (h c) -> p h c", h=HEADS)
                dve.wait_ge(tr1_ps, QT * b + qt + 1)
                link(nc.vector.reciprocal(rden[:], o[:, :, DH]))
                nc.vector.tensor_tensor(on[:, qt, :].rearrange("p (h d) -> p h d", h=HEADS), o[:, :, 0:DH],
                                        rden[:].unsqueeze(2).broadcast_to([P, HEADS, DH]),
                                        ALU.mult).then_inc(on_ok, 1)

            def split_o(b):
                dve.wait_ge(ohi_ok, b + 1)
                nc.vector.tensor_tensor(olo[:], ps_wk, ohi[:].bitcast(F32), ALU.subtract).then_inc(olo_ok, 1)

            def residual(b):
                dve.wait_ge(wo_ps, b + 1)
                dve.wait_ge(xb_ok, b + 1)
                ga = gates[:, GA, b, :].unsqueeze(1).broadcast_to([P, QT, D])
                link(nc.vector.tensor_tensor(on[:], ps_wk, ga, ALU.mult))
                s = xs[:, QT * b:QT * b + QT, :]
                nc.vector.tensor_tensor(s, on[:], s, ALU.add).then_inc(x2_ok, 1)
                dve.wait_ge(x2_ok, b + 1)
                variance(1, b)

            def normalise2(b):
                dve.wait_ge(gates_in, 64)
                dve.wait_ge(rstd_ok, B + b + 1)
                if b:
                    dve.wait_ge(h2_out, 16 * b)
                    dve.wait_ge(h2T_ps, b)
                for t in range(QT):
                    i = QT * b + t
                    last = nc.vector.scalar_tensor_tensor(out=h2r[:, t, :], in0=xs[:, i, :], scalar=mv[:, 1, i, 0:1],
                                                          in1=gates[:, CB1, b, :], op0=ALU.subtract, op1=ALU.mult)
                link(last)
                for t in range(QT):
                    i = QT * b + t
                    last = nc.vector.scalar_tensor_tensor(out=h2r[:, t, :], in0=h2r[:, t, :], scalar=rstd[:, 1, i:i + 1],
                                                          in1=gates[:, SBI, b, :], op0=ALU.mult, op1=ALU.add)
                last.then_inc(h2_ok, 1)

            def choose(b):
                dve.wait_ge(lg_ps, b + 1)
                last = nc.vector.tensor_copy(lg[:], ps_w[:, 0:QT * NE].rearrange("p (t e) -> p t e", t=QT))
                last.then_inc(lg_ok, 1)
                dve.wait_ge(lg_ok, b + 1)
                for t in range(QT):
                    link(nc.vector.max(m8[:, t, :], lg[:, t, :]))
                    link(nc.vector.max_index(i8[:, t, :], m8[:, t, :], lg[:, t, :]))
                nc.vector.tensor_tensor(dlt[:], m8[:, :, 1], m8[:, :, 0], ALU.subtract).then_inc(dlt_ok, 1)
                link(nc.vector.tensor_copy(e12[:], i8[:, :, 0:2]))
                for t in range(QT):
                    last = nc.vector.tensor_tensor(hot[:, t], iota8[:].unsqueeze(1).broadcast_to([P, 2, NE]),
                                                   e12[:, t, :].unsqueeze(2).broadcast_to([P, 2, NE]), ALU.is_equal)
                    link(last)
                nc.vector.tensor_tensor(picked[:, QT * b:QT * b + QT, :], hot[:, :, 0, :], hot[:, :, 1, :],
                                        ALU.add).then_inc(picked_ok, 1)

            def weigh(b):
                dve.wait_ge(edlt_ok, b + 1)
                if b:
                    dve.wait_ge(routed, 64 * b)
                nc.vector.tensor_copy(info[:, :, TOK], token[:, QT * b:QT * b + QT])
                nc.vector.tensor_copy(info[:, :, E1], e12[:, :, 0])
                link(nc.vector.tensor_scalar(wsum[:], edlt[:], 1.0, None, ALU.add))
                link(nc.vector.reciprocal(wsum[:], wsum[:]))
                link(nc.vector.tensor_tensor(info[:, :, W2], edlt[:], wsum[:], ALU.mult))
                link(nc.vector.tensor_tensor(info[:, :, DW], wsum[:], info[:, :, W2], ALU.subtract))

            def place(b):
                dve.wait_ge(rank_ps, b + 1)
                nc.vector.tensor_tensor(pos[:], ps_w[:, 0:QT * NE].rearrange("p (t e) -> p t e", t=QT),
                                        region[:].unsqueeze(1).broadcast_to([P, QT, NE]), ALU.add).then_inc(pos_ok, 1)
                dve.wait_ge(pos_ok, b + 1)
                for t in range(QT):
                    link(nc.vector.tensor_tensor(hot[:, t], hot[:, t], pos[:, t, :].unsqueeze(1).broadcast_to([P, 2, NE]),
                                                 ALU.mult))
                link(nc.vector.tensor_reduce(slotf[:], hot[:], AX.X, ALU.add))
                link(nc.vector.tensor_copy(slot_n[:], slotf[:]))
                link(nc.vector.tensor_scalar(slot_b[:], slot_n[:], 7, None, ALU.logical_shift_right))
                link(nc.vector.tensor_scalar(slot_p[:], slot_n[:], P - 1, None, ALU.bitwise_and))
                nc.vector.scalar_tensor_tensor(out=slot[:], in0=slot_p[:], scalar=float(NB), in1=slot_b[:],
                                               op0=ALU.mult, op1=ALU.add).then_inc(slot_ok, 1)

            def plan():
                def per_tile(t):
                    return t[:].unsqueeze(2).broadcast_to([P, NT, NE])

                def per_expert(t, n=NT):
                    return t[:].unsqueeze(1).broadcast_to([P, n, NE])

                dve.wait_ge(count_ps, 1)
                link(nc.vector.tensor_copy(count[:], ps_w[:, 0:NE]))
                link(nc.vector.tensor_tensor(prod[:, 0:NE, :], count[:].unsqueeze(2).broadcast_to([P, NE, NE]),
                                             per_expert(steps, NE), ALU.is_gt))
                link(nc.vector.tensor_reduce(tiles[:], prod[:, 0:NE, :], AX.X, ALU.add))
                link(nc.vector.tensor_tensor_scan(tend[:], ones8[:], tiles[:], 0.0, ALU.mult, ALU.add))
                link(nc.vector.tensor_tensor(tbeg[:], tend[:], tiles[:], ALU.subtract))
                link(nc.vector.tensor_tensor(prod[:], per_expert(tend), per_tile(tile_no), ALU.is_le))
                link(nc.vector.tensor_reduce(texp[:], prod[:], AX.X, ALU.add))
                link(nc.vector.tensor_scalar(texp[:], texp[:], NE - 1.0, None, ALU.min))
                link(nc.vector.tensor_copy(texp_i[:], texp[:]))
                link(nc.vector.tensor_tensor(pick[:], per_expert(iota8), per_tile(texp), ALU.is_equal))
                link(nc.vector.tensor_tensor(prod[:], pick[:], per_expert(tbeg), ALU.mult))
                link(nc.vector.tensor_reduce(tbase[:], prod[:], AX.X, ALU.add))
                link(nc.vector.tensor_tensor(tblock[:], tile_no[:], tbase[:], ALU.subtract))
                link(nc.vector.scalar_tensor_tensor(out=tblock[:], in0=texp[:], scalar=float(T), in1=tblock[:],
                                                    op0=ALU.mult, op1=ALU.add))
                nc.vector.tensor_scalar(tblock_i[:], tblock[:], NB - 1.0, None, ALU.min).then_inc(plan_ok, 1)

            def weigh_all():
                dve.wait_ge(entries_in, 16)
                nc.vector.tensor_copy(tok[:], entries[:, :, TOK]).then_inc(tok_ok, 1)
                link(nc.vector.tensor_tensor(wgt[:], entries[:, :, E1], block_expert[:], ALU.is_equal))
                link(nc.vector.tensor_tensor(wgt[:], wgt[:], entries[:, :, DW], ALU.mult))
                nc.vector.tensor_tensor(wgt[:], wgt[:], entries[:, :, W2], ALU.add).then_inc(wgt_ok, 1)

            def split_weights(i, s):
                dve.wait_ge(whi_ok, i + 1)
                nc.vector.tensor_tensor(wlo[:, s], w_raw[:, s], whi[:, s].bitcast(F32),
                                        ALU.subtract).then_inc(wsplit_ok, 1)

            dve.wait_ge(x_in[0], 16)
            variance(0, 0)
            normalise(0)
            dve.wait_ge(mod_ps, 1)
            nc.vector.tensor_copy(mrow[0:B, :], ps_s[0][0:B].rearrange("p a b -> p (a b)")).then_inc(mrow_ok, 1)
            dve.wait_ge(modT_ps, 1)
            nc.vector.tensor_copy(modT[:, 0:2, :], ps_s[1][:, 0, 0:2 * B].rearrange("p (j b) -> p j b", j=2))
            nc.vector.tensor_scalar(modT[:, 2:4, :], ps_s[1][:, 0, 2 * B:4 * B].rearrange("p (j b) -> p j b", j=2),
                                    1.0, None, ALU.add).then_inc(modT_ok, 1)
            split_weights(0, slice(0, 3))
            split_h(0)
            dve.wait_ge(x_in[1], 16)
            variance(0, 1)
            normalise(1)
            keep_qkv(0)
            split_h(1)
            split_weights(1, slice(3, 4))
            keep_qkv(1)
            dve.wait_ge(mrow23_ok, 2)
            cb = mrow[64:64 + B, 0:D]
            nc.vector.tensor_scalar(cb, cb, 1.0, None, ALU.add)
            for r, c in ((32, 0), (64, D)):
                g, s, a = mrow[r:r + B, c:c + D], gsign[r:r + B, :], gabs[r:r + B, :]
                link(nc.vector.tensor_scalar(s, g, 0.0, 2.0, ALU.is_ge, ALU.mult))
                link(nc.vector.scalar_tensor_tensor(out=a, in0=s, scalar=-1.0, in1=g, op0=ALU.add, op1=ALU.mult))
                link(nc.vector.tensor_scalar(a, a, 0.25, None, ALU.max))
                nc.vector.scalar_tensor_tensor(out=g, in0=s, scalar=-1.0, in1=a, op0=ALU.add,
                                               op1=ALU.mult).then_inc(gate_rows, 1)
            for b in range(2, B):
                dve.wait_ge(x_in[b], 16)
                variance(0, b)
            for u in range(16):
                row_max(0, u)
            maxima(0)
            for b in range(B):
                if b + 2 < B:
                    normalise(b + 2)
                    split_h(b + 2)
                    keep_qkv(b + 2)
                for u in range(16):
                    if b + 1 < B:
                        row_max(b + 1, u)
                    if b:
                        if u in (1, 3):
                            divide(b - 1, u // 2)
                        elif u == 5:
                            split_o(b - 1)
                        elif u == 7:
                            residual(b - 1)
                        elif u == 9:
                            normalise2(b - 1)
                        elif u == 13:
                            choose(b - 1)
                        elif u == 15:
                            weigh(b - 1)
                            place(b - 1)
                if b + 1 < B:
                    maxima(b + 1)
            for qt in range(QT):
                divide(B - 1, qt)
            split_o(B - 1)
            residual(B - 1)
            normalise2(B - 1)
            choose(B - 1)
            weigh(B - 1)
            place(B - 1)
            plan()
            weigh_all()

            def gate_up(i, par):
                j = 2 * i + par
                dve.wait_ge(act0_ok, j + 1)
                nc.vector.tensor_tensor(inter[par][:], ps_h[par][:, 1, :], act0[par][:], ALU.mult).then_inc(inter_ok, 1)

            def keep_i(i, par):
                j = 2 * i + par
                dve.wait_ge(i_ps, j + 1)
                nc.vector.tensor_copy(iT[par][:].rearrange("p m t -> p (m t)"), ps_i).then_inc(iT_ok, 1)

            dve.sem_inc(inter_ok, 2)
            dve.sem_inc(iT_ok, 1)
            gate_up(0, 0)
            with dve.Fori(0, (NT - 1) // 2) as i:
                for par in range(2):
                    keep_i(i, par)
                    gate_up(i + par, 1 - par)
            keep_i((NT - 1) // 2, 0)

            for b in range(B):
                a = acc[:, QT * b:QT * b + QT, :]
                dve.wait_ge(acc_in[b], 16)
                link(nc.vector.tensor_tensor(a, a, gates[:, GB, b, :].unsqueeze(1).broadcast_to([P, QT, D]), ALU.mult))
                nc.vector.tensor_tensor(a, a, xs[:, QT * b:QT * b + QT, :], ALU.add).then_inc(res_ok, 1)

        @block.tensor
        def _(pe):
            w_reader = [None]

            def take_w():
                if w_reader[0]:
                    pe.wait_ge(*w_reader[0])

            def three(out, stat, mov, first, last):
                for i, (s, m) in enumerate(((stat[0], mov[0]), (stat[0], mov[1]), (stat[1], mov[0]))):
                    ins = nc.tensor.matmul(out, s, m, start=first and i == 0, stop=last and i == 2)
                return ins

            def h_columns(b):
                pe.wait_ge(h1n_ok, b + 1)
                take_w()
                for k in range(KC):
                    for t in range(QT):
                        last = nc.tensor.transpose(ps_wk[:, k, P * t:P * t + P], h1n[:, t, P * k:P * k + P], ident[:])
                last.then_inc(hT_ps, 1)
                w_reader[0] = (hT_ok, KC * (b + 1))

            def project(b):
                pe.wait_ge(wsplit_ok, 1)
                pe.wait_ge(h_ok, b + 1)
                if b >= 3:
                    pe.wait_ge(exp_ok, NG * (b - 2))
                elif b >= 1:
                    pe.wait_ge(klo_ok, b)
                for i, done in enumerate((q_ps, k_ps)):
                    for m in range(KC):
                        for k in range(KC):
                            c = slice(P * m, P * m + P)
                            last = three(ps_qk[i][:, m, :], (whi[:, i, k, c], wlo[:, i, k, c]),
                                         (hhi[:, k, :], hlo[:, k, :]), k == 0, k == KC - 1)
                    last.then_inc(done, 1)
                if b in (1, 2):
                    pe.wait_ge(va_ok, b)
                for t in range(QT):
                    for k in range(KC):
                        c = slice(P * t, P * t + P)
                        last = three(ps_v[:, t, :], (hhi[:, k, c], hlo[:, k, c]),
                                     (whi[:, 2, k, :], wlo[:, 2, k, :]), k == 0, k == KC - 1)
                last.then_inc(v_ps, 1)

            def score(b, u):
                p, hp, qt, gg = b % 2, u % 2, u // 8, u // 2 % 4
                if u == 0:
                    pe.wait_ge(stack_in[p], 12 * 16 * (b // 2 + 1))
                if 16 * b + u >= 2:
                    pe.wait_ge(mx_ok, 16 * b + u - 1)
                r = HR * hp
                for i in range(2):
                    g = 2 * gg + i
                    last = nc.tensor.matmul(ps_s[hp][:, i, :], qs[r:r + K_MAX, p, g, P * qt:P * qt + P],
                                            ks[r:r + K_MAX, p, g, :], start=True, stop=True)
                last.then_inc(s_ps, 1)

            def maxima(b):
                pe.wait_ge(mx_ok, 16 * (b + 1))
                take_w()
                for qt in range(QT):
                    last = nc.tensor.transpose(ps_w[0:HEADS, P * qt:P * qt + P], mx[:, b % 2, qt, :], ident[:])
                last.then_inc(mT_ps, 1)
                w_reader[0] = (mlo_ok, b + 1)

            def score_T(b, g):
                p, u = b % 2, NG * b + g
                if g == 0:
                    pe.wait_ge(m_in[p], landed(b))
                    done = min(b + 3, B)
                    pe.wait_ge(klo_ok, done)
                    pe.wait_ge(va_ok, done)
                if u >= 2:
                    pe.wait_ge(exp_ok, u - 1)
                for hp in range(2):
                    r = HR * hp
                    for kc in range(QT):
                        last = nc.tensor.matmul(ps_t[g % 2][:, hp, L * kc:L * kc + L],
                                                ks[r:r + K_SUB, p, g, P * kc:P * kc + P],
                                                qs[r:r + K_SUB, p, g, :], start=True, stop=True)
                last.then_inc(t_ps, 1)

            def weighted(b, n):
                pe.wait_ge(exp_ok, NG * b + 2 * n + 2)
                if n % 2 == 0 and 4 * b + n:
                    pe.wait_ge(oT_ok, 2 * b + n // 2)
                for kc in range(QT):
                    for h in range(4 * n, 4 * n + 4):
                        r = 32 * (h % 4)
                        last = nc.tensor.matmul(ps_pv[r:r + 32, n % 2, :], va[:, b % 3, kc, h, :],
                                                probs[:, h // 2 % 4, h % 2, L * kc:L * kc + L],
                                                start=kc == 0, stop=kc == QT - 1)
                last.then_inc(pv_ps, 1)

            def o_rows(b, qt):
                pe.wait_ge(oT_ok, 2 * (b + 1))
                take_w()
                for n in range(HEADS // 4):
                    last = nc.tensor.transpose(ps_w[:, P * n:P * n + P], oT[:, n, P * qt:P * qt + P], ident[:])
                last.then_inc(tr1_ps, 1)
                w_reader[0] = (on_ok, QT * b + qt + 1)

            def o_columns(b):
                pe.wait_ge(on_ok, QT * (b + 1))
                take_w()
                for k in range(KC):
                    for qt in range(QT):
                        last = nc.tensor.transpose(ps_wk[:, k, P * qt:P * qt + P], on[:, qt, P * k:P * k + P], ident[:])
                last.then_inc(tr2_ps, 1)
                w_reader[0] = (olo_ok, b + 1)

            def project_o(b):
                pe.wait_ge(olo_ok, b + 1)
                take_w()
                pe.wait_ge(wsplit_ok, 2)
                for qt in range(QT):
                    for k in range(KC):
                        c = slice(P * qt, P * qt + P)
                        last = three(ps_wk[:, qt, :], (ohi[:, k, c], olo[:, k, c]),
                                     (whi[:, 3, k, :], wlo[:, 3, k, :]), k == 0, k == KC - 1)
                last.then_inc(wo_ps, 1)
                w_reader[0] = (x2_ok, b + 1)

            def h2_columns(b):
                pe.wait_ge(h2_ok, b + 1)
                take_w()
                for k in range(KC):
                    for t in range(QT):
                        last = nc.tensor.transpose(ps_wk[:, k, P * t:P * t + P], h2r[:, t, P * k:P * k + P], ident[:])
                last.then_inc(h2T_ps, 1)
                w_reader[0] = (h2T_ok, b + 1)

            def logits(b):
                take_w()
                for t in range(QT):
                    for k in range(KC):
                        last = nc.tensor.matmul(ps_w[:, NE * t:NE * t + NE], h2T[:, k, P * t:P * t + P],
                                                gate_sb[:, k, :], start=k == 0, stop=k == KC - 1)
                last.then_inc(lg_ps, 1)
                w_reader[0] = (lg_ok, b + 1)

            def ranks(b):
                pe.wait_ge(picked_ok, b + 1)
                pe.wait_ge(const_ok, 1)
                take_w()
                for t in range(QT):
                    i = QT * b + t
                    for n in range(i + 1):
                        last = nc.tensor.matmul(ps_w[:, NE * t:NE * t + NE], upper[:] if n == i else ones_bf[:],
                                                picked[:, n, :], start=n == 0, stop=n == i)
                last.then_inc(rank_ps, 1)
                w_reader[0] = (pos_ok, b + 1)

            pe.wait_ge(ident_ok, 1)
            h_columns(0)

            def modulation(thirds):
                for k in range(KC):
                    for n in thirds:
                        last = nc.tensor.matmul(ps_s[0][32 * n:32 * n + B].rearrange("p a b -> p (a b)"), sc[:, k, :],
                                                wmod_sb[:, k, 2 * D * n:2 * D * n + 2 * D],
                                                start=k == 0, stop=k == KC - 1)
                last.then_inc(mod_ps, 1)

            pe.wait_ge(silu_ok, 1)
            pe.wait_ge(wmod_in[0], 16)
            modulation((0,))
            pe.wait_ge(mrow_ok, 1)
            for j in range(4):
                last = nc.tensor.transpose(ps_s[1][:, 0, B * j:B * j + B], mrow[0:B, P * j:P * j + P], ident[0:B, 0:B])
            last.then_inc(modT_ps, 1)
            project(0)
            h_columns(1)
            pe.wait_ge(wmod_in[1], 32)
            modulation((1, 2))
            project(1)
            pe.wait_ge(mrow23_ok, 2)
            for u in range(16):
                score(0, u)
            maxima(0)
            for b in range(B):
                if b + 2 < B:
                    h_columns(b + 2)
                    project(b + 2)
                for g in range(NG):
                    if g:
                        score_T(b, g)
                    if b + 1 < B:
                        score(b + 1, 2 * g)
                        score(b + 1, 2 * g + 1)
                    if g in (2, 4, 6):
                        weighted(b, g // 2 - 1)
                    if b:
                        if g < QT:
                            o_rows(b - 1, g)
                        elif g == 2:
                            o_columns(b - 1)
                        elif g == 3:
                            project_o(b - 1)
                        elif g == 5:
                            h2_columns(b - 1)
                        elif g == 6:
                            logits(b - 1)
                        elif g == 7:
                            ranks(b - 1)
                    if g == 0:
                        score_T(b, g)
                if b + 1 < B:
                    maxima(b + 1)
                weighted(b, 3)
            for qt in range(QT):
                o_rows(B - 1, qt)
            o_columns(B - 1)
            project_o(B - 1)
            h2_columns(B - 1)
            logits(B - 1)
            ranks(B - 1)
            take_w()
            for n in range(T):
                last = nc.tensor.matmul(ps_w[:, 0:NE], ones_bf[:], picked[:, n, :], start=n == 0, stop=n == T - 1)
            last.then_inc(count_ps, 1)

            def columns_x(i, par):
                j = 2 * i + par
                pe.wait_ge(xg_in[par], 16 * i + 16)
                pe.wait_ge(xT_ok, j)
                for k in range(KC):
                    last = nc.tensor.transpose(ps_x[:, k, :], xg[par][:, P * k:P * k + P], ident[:])
                last.then_inc(x_ps, 1)

            def expert(i, par):
                return pe.value_load(texp_i[0:1, bass.ds(2 * i + par, 1)], min_val=0, max_val=NE - 1)

            def hidden(i, par, e):
                j = 2 * i + par
                pe.wait_ge(xT_ok, j + 1)
                pe.wait_ge(inter_ok, j + 1)
                for n in range(2):
                    for k in range(KC):
                        last = nc.tensor.matmul(ps_h[par][:, n, :], xT[par][:, k, :],
                                                w01[:, bass.ds(e, 1), k, F * n:F * n + F],
                                                start=k == 0, stop=k == KC - 1)
                last.then_inc(hid_ps, 1)

            def columns_i(i, par):
                j = 2 * i + par
                pe.wait_ge(inter_ok, j + 3)
                pe.wait_ge(iT_ok, j + 1)
                for m in range(FC):
                    last = nc.tensor.transpose(ps_i[:, P * m:P * m + P], inter[par][:, P * m:P * m + P], ident[:])
                last.then_inc(i_ps, 1)

            def down(i, par, e):
                j = 2 * i + par
                pe.wait_ge(iT_ok, j + 2)
                pe.wait_ge(ys_ok, j + 1)
                for m in range(FC):
                    last = nc.tensor.matmul(ps_y[par], iT[par][:, m, :], wex[:, bass.ds(e, 1), m, :],
                                            start=m == 0, stop=m == FC - 1)
                last.then_inc(y_ps, 1)

            pe.wait_ge(plan_ok, 1)
            pe.wait_ge(oT_ok, 2 * B)
            columns_x(0, 0)
            columns_x(0, 1)
            pe.wait_ge(w01_in, 16 * 2 * NE)
            hidden(0, 0, expert(0, 0))
            pe.wait_ge(wex_in, 16 * NE)
            with pe.Fori(0, (NT - 3) // 2) as i:
                e = [expert(i, 0), expert(i, 1), expert(i + 1, 0)]
                for par in range(2):
                    columns_i(i, par)
                    hidden(i + par, 1 - par, e[par + 1])
                    columns_x(i + 1, par)
                    down(i, par, e[par])
            n = (NT - 3) // 2
            e = [expert(n, 0), expert(n, 1), expert(n + 1, 0)]
            columns_i(n, 0)
            hidden(n, 1, e[1])
            columns_x(n + 1, 0)
            down(n, 0, e[0])
            columns_i(n, 1)
            hidden(n + 1, 0, e[2])
            down(n, 1, e[1])
            columns_i(n + 1, 0)
            down(n + 1, 0, e[2])


def kernel(**inputs):
    import numpy as np
    import concourse.bacc as bacc
    from concourse.bass_utils import run_bass_kernel_spmd

    nc = bacc.Bacc("TRN2", target_bir_lowering=False, num_devices=1)
    given = {n: np.asarray(a) for n, a in inputs.items()}
    names = ["L0_attn_x", "L0_attn_Wq", "L0_attn_bq", "L0_attn_Wk", "L0_attn_bk", "L0_attn_Wv", "L0_attn_bv",
             "L0_attn_Wo", "L0_attn_bo", "L0_ffn_gate_kernel", "L0_ffn_w0_kernel", "L0_ffn_w1_kernel",
             "L0_ffn_wo_kernel", "L0_c", "L0_wmod"]
    given["L0_c"] = given["L0_c"].T
    for n in ("L0_attn_bq", "L0_attn_bk"):
        given[n] = given[n].reshape(KC, P).T
    arrays, args = {}, []
    for n in names:
        a = np.ascontiguousarray(given[n])
        arrays[n] = a
        args.append(nc.dram_tensor(n, a.shape, mybir.dt.from_np(a.dtype), kind="ExternalInput").ap())
    out = nc.dram_tensor("out", (B, L, D), F32, kind="ExternalOutput").ap()
    adaln_block(nc, *args, out)
    r = run_bass_kernel_spmd(nc, [arrays], core_ids=[0])
    return r.results[0]["out"]
```

```python
from contextlib import ExitStack

import concourse.bass as bass
from concourse import mybir

F32 = mybir.dt.float32
F32R = mybir.dt.float32r
BF16 = mybir.dt.bfloat16
I32 = mybir.dt.int32
U32 = mybir.dt.uint32
ALU = mybir.AluOpType
ACT = mybir.ActivationFunctionType
AX = mybir.AxisListType

P = 128
B, L, D = 4, 256, 256
HEADS, DH = 16, 16
NE, F = 8, 512
KC = D // P
QT = L // P
T = B * QT
NG = HEADS // 2
HR = 64
K_MAX = 3 * DH
K_SUB = K_MAX + 2
FC = F // P
NT = (2 * B * L + NE * (P - 1)) // P
NA = -(-(2 * (B - 1) * L - NE * (P - 1)) // P)
NB = NE * B * L // P + 1
TOK, WGT, ENT = 0, 1, 4
EPS = 1e-5


def adaln_block(nc, x, wq, bq, wk, bk, wv, bv, wo, bo, gate, w0, w1, wout, cT, wmod, out):
    ctx = ExitStack()
    with ctx:
        top = [16512]

        def at(name, shape, dt, offset):
            return nc.alloc_sbuf_tensor_at(name, shape, dt, offset=offset)

        def sb(name, shape, dt):
            n = 4 if dt != BF16 else 2
            for s in shape[1:]:
                n *= s
            t = at(name, shape, dt, top[0])
            top[0] += (n + 31) // 32 * 32
            return t

        def sem(name):
            return ctx.enter_context(nc.semaphore(name))

        w01 = sb("w01", [P, NE, KC, 2 * F], F32)
        late = top[0]
        wex = sb("wex", [P, NE, FC, D], F32)
        probs = at("probs", [P, 4, 2, QT * L], F32, late)
        wmod_sb = at("wmod_sb", [P, KC, 6 * D], F32, late + 16384)
        h1n = at("h1n", [P, QT, D], F32, late + 28672)
        hT = at("hT", [P, KC, L], F32, late + 30720)
        xs = sb("xs", [P, T, D], F32)
        gates = sb("gates", [P, 4, B, D], F32)
        w_raw = at("w_raw", [P, 4, KC, D], F32, top[0] - 8192)
        GA, SBI, CB1, GB = range(4)
        bv_b = sb("bv_b", [P, D], F32)
        bo_b = sb("bo_b", [P, D], F32)
        gbo = sb("gbo", [P, D], F32)
        ident = sb("ident", [P, P], F32)
        bqk = sb("bqk", [P, 2, KC], F32)
        gate_sb = sb("gate_sb", [P, KC, NE], F32)
        cT_sb = sb("cT_sb", [P, KC, B], F32)
        sc = sb("sc", [P, KC, B], F32)
        modT = sb("modT", [P, 4, B], F32)
        mrow = sb("mrow", [P, 2 * D], F32)
        gsign = at("gsign", [P, D], F32, late + 16384)
        gabs = at("gabs", [P, D], F32, late + 17408)
        stats = sb("stats", [P, QT, 6], F32)
        mv = sb("mv", [P, 2, T, 2], F32)
        veps = sb("veps", [P, 2, T], F32)
        rstd = sb("rstd", [P, 2, T], F32)
        mhalf = sb("mhalf", [P, QT], F32)
        mx = sb("mx", [P, 2, QT, HEADS], F32)
        attn_at = top[0]
        whi = sb("whi", [P, 4, KC, D], F32R)
        wlo = sb("wlo", [P, 4, KC, D], F32R)
        stack_at = top[0]
        qs = sb("qs", [P, 2, NG, L], F32R)
        ks = sb("ks", [P, 2, NG, L], F32R)
        va = sb("va", [P, 3, QT, HEADS, 32], F32)
        hhi = sb("hhi", [P, KC, L], F32R)
        hlo = sb("hlo", [P, KC, L], F32R)
        qk = sb("qk", [P, 4, KC, L], F32R)
        mneg = sb("mneg", [HEADS, 2, L], F32R)
        stack_end = top[0]
        oT = at("oT", [P, HEADS // 4, L], F32, late + 16384)
        on = at("on", [P, QT, D], F32, late + 20480)
        ohi = at("ohi", [P, KC, L], F32R, late + 22528)
        olo = at("olo", [P, KC, L], F32R, late + 24576)
        rden = sb("rden", [P, HEADS], F32)
        h2r = sb("h2r", [P, QT, D], F32)
        info = sb("info", [P, QT, 2, ENT], I32)
        pad_info = sb("pad_info", [P, NB, ENT], I32)
        h2T = sb("h2T", [P, KC, L], F32)
        iota8 = sb("iota8", [P, NE], F32)
        region = sb("region", [P, NE], F32)
        ones8 = sb("ones8", [P, NE], F32)
        part_no = sb("part_no", [P, 1], F32)
        token = sb("token", [P, T], I32)
        upper = sb("upper", [P, P], BF16)
        ones_bf = sb("ones_bf", [P, P], BF16)
        lg = sb("lg", [P, QT, NE], F32)
        m8 = sb("m8", [P, QT, 8], F32)
        i8 = sb("i8", [P, QT, 8], U32)
        dlt = sb("dlt", [P, QT], F32)
        edlt = sb("edlt", [P, QT], F32)
        wsum = sb("wsum", [P, QT], F32)
        e12 = sb("e12", [P, QT, 2], F32)
        hot = sb("hot", [P, QT, 2, NE], F32)
        picked = sb("picked", [P, T, NE], BF16)
        pos = sb("pos", [P, QT, NE], F32)
        slotf = sb("slotf", [P, QT, 2], F32)
        slot_n = sb("slot_n", [P, QT, 2], U32)
        slot_b = sb("slot_b", [P, QT, 2], U32)
        slot_p = sb("slot_p", [P, QT, 2], U32)
        slot = sb("slot", [P, QT, 2], U32)
        count = sb("count", [P, NE], U32)
        tiles = sb("tiles", [P, NE], F32)
        tend = sb("tend", [P, NE], F32)
        tbeg = sb("tbeg", [P, NE], F32)
        taken = sb("taken", [P, NE], F32)
        pick = sb("pick", [P, NE], F32)
        texp = sb("texp", [P, 1], F32)
        tbase = sb("tbase", [P, 1], F32)
        tblock = sb("tblock", [P, 1], F32)
        assert top[0] <= nc.sbuf_usable_end, top[0]
        top[0] = stack_at
        tblock_i = sb("tblock_i", [1, NT], I32)
        texp_i = sb("texp_i", [1, NT], I32)
        entries = [sb(f"entries{i}", [P, NB, ENT], I32) for i in range(2)]
        tokg = [sb(f"tokg{i}", [P, 1], I32) for i in range(2)]
        toka = [sb(f"toka{i}", [P, 1], I32) for i in range(2)]
        xg = [sb(f"xg{i}", [P, D], F32) for i in range(2)]
        xhi = [sb(f"xhi{i}", [P, KC, P], F32R) for i in range(2)]
        xlo = [sb(f"xlo{i}", [P, KC, P], F32R) for i in range(2)]
        act0 = [sb(f"act0{i}", [P, F], F32) for i in range(2)]
        inter = [sb(f"inter{i}", [P, F], F32) for i in range(2)]
        iT = [sb(f"iT{i}", [P, FC, P], F32) for i in range(2)]
        ys = [sb(f"ys{i}", [P, D], F32) for i in range(2)]
        ehi = [sb(f"ehi{i}", [P, KC, 2 * F], F32R) for i in range(2)]
        elo = [sb(f"elo{i}", [P, KC, 2 * F], F32R) for i in range(2)]
        assert top[0] <= stack_end
        acc = at("acc", [P, T, D], F32, attn_at)

        ps_s = [ctx.enter_context(nc.psum_tensor(f"ps_s{i}", [P, 2, L], F32)) for i in range(2)]
        ps_t = [ctx.enter_context(nc.psum_tensor(f"ps_t{i}", [P, 2, QT * L], F32)) for i in range(2)]
        ps_pv = ctx.enter_context(nc.psum_tensor("ps_pv", [P, 2, L], F32))
        ps_w = ctx.enter_context(nc.psum_tensor("ps_w", [P, 512], F32))
        ps_qk = [ps_t[0][:, i, :].rearrange("p (m t) -> p m t", m=KC) for i in range(2)]
        ps_v = ps_t[1][:, 0, :].rearrange("p (t n) -> p t n", t=QT)
        ps_wk = ps_w[:].rearrange("p (k t) -> p k t", k=2)
        ps_plan = [ps_s[0][:, 0, :], ps_w]
        ps_h = ps_t
        ps_x = ps_s[1][:, 0, :].rearrange("p (k t) -> p k t", k=KC)
        ps_i = ps_pv[:].rearrange("p a b -> p (a b)")
        ps_y = ps_s[0][:, 0, :]

        info_d = nc.dram_tensor("routed", (P * NB, ENT), I32, kind="Internal").ap()
        h2_d = nc.dram_tensor("h2_rows", (B * L + P, D), F32, kind="Internal").ap()
        acc_d = nc.dram_tensor("mixture_sums", (B * L + P, D), F32, kind="Internal").ap()
        scratch = nc.dram_tensor("qk_scratch", (B, 4, D, L), F32, kind="Internal").ap()
        mod_d = nc.dram_tensor("mod_scratch", (4, B, D), F32, kind="Internal").ap()

        x_in = [sem(f"x_in{b}") for b in range(B)]
        c_in = sem("c_in")
        wmod_in = [sem(f"wmod_in{i}") for i in range(2)]
        wraw_in = [sem(f"wraw_in{i}") for i in range(2)]
        whi_ok = sem("whi_ok")
        small_in = sem("small_in")
        ident_ok = sem("ident_ok")
        zero_ok = sem("zero_ok")
        ones_ok = sem("ones_ok")
        dve_chain = sem("dve_chain")
        pool_chain = sem("pool_chain")
        silu_ok = sem("silu_ok")
        mod_ps = sem("mod_ps")
        mrow_ok = sem("mrow_ok")
        mrow23_ok = sem("mrow23_ok")
        gate_rows = sem("gate_rows")
        modT_ps = sem("modT_ps")
        modT_ok = sem("modT_ok")
        mod_out = sem("mod_out")
        gates_in = sem("gates_in")
        wsplit_ok = sem("wsplit_ok")
        var_ok = sem("var_ok")
        rstd_ok = sem("rstd_ok")
        h1n_ok = sem("h1n_ok")
        hT_ps = sem("hT_ps")
        hT_ok = sem("hT_ok")
        h_ok = sem("h_ok")
        q_ps = sem("q_ps")
        k_ps = sem("k_ps")
        v_ps = sem("v_ps")
        qhi_ok = sem("qhi_ok")
        khi_ok = sem("khi_ok")
        qlo_ok = sem("qlo_ok")
        klo_ok = sem("klo_ok")
        va_ok = sem("va_ok")
        q_out = [sem(f"q_out{p}") for p in range(2)]
        k_out = [sem(f"k_out{p}") for p in range(2)]
        stack_in = [sem(f"stack_in{p}") for p in range(2)]
        third_in = [sem(f"third_in{p}") for p in range(2)]
        s_ps = sem("s_ps")
        mx_ok = sem("mx_ok")
        mT_ps = sem("mT_ps")
        mhi_ok = sem("mhi_ok")
        mlo_ok = sem("mlo_ok")
        m_in = [sem(f"m_in{p}") for p in range(2)]
        t_ps = sem("t_ps")
        exp_ok = sem("exp_ok")
        pv_ps = sem("pv_ps")
        oT_ok = sem("oT_ok")
        tr1_ps = sem("tr1_ps")
        on_ok = sem("on_ok")
        tr2_ps = sem("tr2_ps")
        ohi_ok = sem("ohi_ok")
        olo_ok = sem("olo_ok")
        wo_ps = sem("wo_ps")
        xb_ok = sem("xb_ok")
        x2_ok = sem("x2_ok")
        w01_in = sem("w01_in")
        wex_in = sem("wex_in")
        pad_ok = sem("pad_ok")
        pad_out = sem("pad_out")
        const_ok = sem("const_ok")
        h2_ok = sem("h2_ok")
        h2T_ps = sem("h2T_ps")
        h2T_ok = sem("h2T_ok")
        lg_ps = sem("lg_ps")
        lg_ok = sem("lg_ok")
        dlt_ok = sem("dlt_ok")
        edlt_ok = sem("edlt_ok")
        picked_ok = sem("picked_ok")
        rank_ps = sem("rank_ps")
        slot_ok = sem("slot_ok")
        routed = sem("routed")
        count_ps = sem("count_ps")
        plan_ok = sem("plan_ok")
        xg_in = [sem(f"xg_in{i}") for i in range(2)]
        x_ps = sem("x_ps")
        xhi_ok = sem("xhi_ok")
        xlo_ok = sem("xlo_ok")
        ehi_ok = sem("ehi_ok")
        elo_ok = sem("elo_ok")
        hid_ps = sem("hid_ps")
        act0_ok = sem("act0_ok")
        inter_ok = sem("inter_ok")
        i_ps = sem("i_ps")
        tokg_ok = sem("tokg_ok")
        toka_ok = sem("toka_ok")
        entries_in = sem("entries_in")
        h2_out = sem("h2_out")
        pool_waited = sem("pool_waited")
        plan_col = sem("plan_col")
        plan_ps = sem("plan_ps")
        count_ok = sem("count_ok")
        pos_ok = sem("pos_ok")
        iT_ok = sem("iT_ok")
        y_ps = sem("y_ps")
        ys_ok = sem("ys_ok")
        y_added = [sem(f"y_added{i}") for i in range(2)]
        acc_in = [sem(f"acc_in{b}") for b in range(B)]
        res_ok = sem("res_ok")
        pool_res_ok = sem("pool_res_ok")
        out_done = sem("out_done")

        def unloaded(b):
            return 32 * (b // 2 + 1)

        def landed(b):
            return 64 * (b // 2 + 1)

        def stack_part(engine, came, b, rows):
            p = b % 2
            if b >= 2:
                engine.wait_ge(t_ps, NG * (b - 1))
            for dst, kind, row in rows:
                if dst is qs:
                    engine.wait_ge(q_out[p], unloaded(b))
                else:
                    engine.wait_ge(k_out[p], unloaded(b))
                    if b < 2:
                        engine.wait_ge(ones_ok, 2 + p)
                for hp in range(2):
                    r = HR * hp + DH * row
                    src = scratch[b, kind].rearrange("(g h d) t -> h d g t", g=NG, h=2)[hp]
                    engine.dma_start(dst[r:r + DH, p, :, :].bitcast(F32), src).then_inc(came[p], 16)

        block = ctx.enter_context(nc.Block())

        @block.sync
        def _(sp):
            def rows(w):
                return w.rearrange("(k p) n -> p k n", p=P)

            def load_x(b):
                sp.dma_start(xs[:, QT * b:QT * b + QT, :],
                             x[b].rearrange("(t p) d -> p t d", p=P)).then_inc(x_in[b], 16)

            def load_w(i, w):
                sp.dma_start(w_raw[:, i], rows(w)).then_inc(wraw_in[i // 3], 16)

            sp.dma_start(cT_sb[:], rows(cT)).then_inc(c_in, 16)
            load_x(0)
            sp.dma_start(wmod_sb[:, :, 0:2 * D], rows(wmod)[:, :, 0:2 * D]).then_inc(wmod_in[0], 16)
            for i, w in enumerate((wq, wk, wv)):
                load_w(i, w)
            load_x(1)
            sp.dma_start(bqk[:, 0, :], bq).then_inc(small_in, 16)
            sp.dma_start(bqk[:, 1, :], bk).then_inc(small_in, 16)
            sp.dma_start(bv_b[:], bv.partition_broadcast(P)).then_inc(small_in, 16)
            sp.dma_start(bo_b[:], bo.partition_broadcast(P)).then_inc(small_in, 16)
            sp.dma_start(gate_sb[:], rows(gate)).then_inc(small_in, 16)
            for k in range(KC):
                sp.dma_start(wmod_sb[:, k, 2 * D:6 * D], wmod[P * k:P * k + P, 2 * D:6 * D]).then_inc(wmod_in[1], 16)
            load_w(3, wo)
            load_x(2)
            load_x(3)

            def unload(b):
                for i, (ready, done) in enumerate(((qhi_ok, q_out), (qlo_ok, q_out), (khi_ok, k_out), (klo_ok, k_out))):
                    sp.wait_ge(ready, b + 1)
                    sp.dma_start(scratch[b, i].rearrange("(m p) t -> p m t", p=P),
                                 qk[:, i].bitcast(F32)).then_inc(done[b % 2], 16)

            def stack(b):
                stack_part(sp, stack_in, b, ((qs, 0, 0), (qs, 0, 1), (ks, 2, 0), (ks, 3, 1)))

            def maxima(b):
                p = b % 2
                for i, ready in enumerate((mhi_ok, mlo_ok)):
                    sp.wait_ge(ready, b + 1)
                    for hp in range(2):
                        r = HR * hp + K_MAX + i
                        sp.dma_start(qs[r:r + 1, p, :, :].bitcast(F32),
                                     mneg[NG * hp:NG * hp + NG, i, :].bitcast(F32)).then_inc(m_in[p], 16)

            def experts(first, n):
                for e in range(first, first + n):
                    for i, w in enumerate((w0, w1)):
                        sp.dma_start(w01[:, e, :, F * i:F * i + F], rows(w[e])).then_inc(w01_in, 16)

            unload(0)
            stack(0)
            unload(1)
            stack(1)
            unload(2)
            maxima(0)
            sp.wait_ge(pad_ok, 2)
            sp.dma_start(acc_d.rearrange("(t p) d -> p t d", p=P),
                         h2T[:, 0, :].unsqueeze(1).broadcast_to([P, T + 1, D])).then_inc(pad_out, 16)
            sp.dma_start(h2_d[B * L:B * L + P], h2T[:, 0, :]).then_inc(pad_out, 16)
            sp.dma_start(info_d.rearrange("(p r) c -> p r c", p=P), pad_info[:]).then_inc(pad_out, 16)

            sp.wait_ge(gate_rows, 2)
            for i, (r, c) in ((GA, (32, 0)), (SBI, (32, D)), (CB1, (64, 0)), (GB, (64, D))):
                sp.dma_start(mod_d[i], mrow[r:r + B, c:c + D]).then_inc(mod_out, 16)
            sp.wait_ge(mod_out, 64)
            sp.wait_ge(wsplit_ok, 2)
            for i in range(4):
                sp.dma_start(gates[:, i], mod_d[i].partition_broadcast(P)).then_inc(gates_in, 16)
            for b in range(B):
                if b == 1:
                    unload(3)
                experts(2 * b, 2)
                if b + 2 < B:
                    stack(b + 2)
                if b + 1 < B:
                    maxima(b + 1)
            for e in range(NE):
                if e == 0:
                    sp.wait_ge(pv_ps, 4 * B)
                if e == NE // 2:
                    sp.wait_ge(x2_ok, B)
                sp.dma_start(wex[:, e], wout[e].rearrange("(m p) d -> p m d", p=P)).then_inc(wex_in, 16)
            sp.wait_ge(y_added[0], 16 * ((NT + 1) // 2))
            sp.wait_ge(y_added[1], 16 * (NT // 2))
            for b in range(B):
                sp.dma_start(acc[:, QT * b:QT * b + QT, :],
                             acc_d[L * b:L * b + L].rearrange("(t p) d -> p t d", p=P)).then_inc(acc_in[b], 16)
            for b in range(B):
                if b == B - 2:
                    sp.wait_ge(pool_res_ok, 1)
                else:
                    sp.wait_ge(res_ok, min(b + 1, B - 1))
                sp.dma_start(out[b].rearrange("(t p) d -> p t d", p=P),
                             acc[:, QT * b:QT * b + QT, :]).then_inc(out_done, 16)
            sp.wait_ge(out_done, 16 * B)

        @block.gpsimd
        def _(pool):
            chain = [0]

            def link(ins):
                chain[0] += 1
                ins.then_inc(pool_chain, 1)
                pool.wait_ge(pool_chain, chain[0])

            link(nc.gpsimd.memset(ident[:], 0.0))
            nc.gpsimd.affine_select(out=ident[:], in_=ident[:], compare_op=ALU.not_equal, fill=1.0, base=0,
                                    pattern=[[-1, P]], channel_multiplier=1).then_inc(ident_ok, 1)
            def rsqrt(ln, b):
                pool.wait_ge(var_ok, B * ln + b + 1)
                s = slice(QT * b, QT * b + QT)
                nc.gpsimd.tensor_tensor(rstd[:, ln, s], veps[:, ln, s], mhalf[:], ALU.pow).then_inc(rstd_ok, 1)

            def stack(b):
                stack_part(pool, third_in, b, ((qs, 1, 2), (ks, 2, 2)))

            link(nc.gpsimd.memset(mhalf[:], -0.5))
            rsqrt(0, 0)
            nc.gpsimd.memset(va[:], 1.0).then_inc(ones_ok, 1)
            rsqrt(0, 1)
            for p in range(2):
                nc.gpsimd.memset(ks[:, p].bitcast(F32), 1.0).then_inc(ones_ok, 1)

            for t, pattern, base, mult in ((iota8[:], [[1, NE]], 0, 0), (region[:], [[B * L, NE]], 0, 0),
                                           (part_no[:], [[0, 1]], 0, 1), (token[:], [[P, T]], 0, 1)):
                nc.gpsimd.iota(t, pattern, base=base, channel_multiplier=mult, allow_small_or_imprecise_dtypes=True)
            link(nc.gpsimd.memset(upper[:], 1.0))
            nc.gpsimd.affine_select(out=upper[:], in_=upper[:], compare_op=ALU.is_gt, fill=0.0, base=0,
                                    pattern=[[1, P]], channel_multiplier=-1)
            nc.gpsimd.memset(info[:], 0)
            nc.gpsimd.memset(ones8[:], 1.0)
            nc.gpsimd.memset(ones_bf[:], 1.0).then_inc(const_ok, 1)
            link(nc.gpsimd.memset(pad_info[:], 0))
            nc.gpsimd.iota(pad_info[:, :, TOK], [[0, NB]], base=B * L, channel_multiplier=1).then_inc(pad_ok, 1)
            nc.gpsimd.memset(h2T[:], 0.0).then_inc(pad_ok, 1)

            stack(0)
            rsqrt(0, 2)
            stack(1)
            rsqrt(0, 3)
            pool.wait_ge(gates_in, 64)
            pool.wait_ge(small_in, 80)
            for b in range(B):
                link(nc.gpsimd.tensor_tensor(gbo[:], bo_b[:], gates[:, GA, b, :], ALU.mult))
                pool.wait_ge(h1n_ok, b + 1)
                for t in range(QT):
                    last = nc.gpsimd.tensor_tensor(xs[:, QT * b + t, :], xs[:, QT * b + t, :], gbo[:], ALU.add)
                    link(last)
                pool.sem_inc(xb_ok, 1)
                if b == 1:
                    stack(2)

            def keep_h2(b):
                pool.wait_ge(h2_ok, b + 1)
                pool.dma_start(h2_d[L * b:L * b + L].rearrange("(t p) d -> p t d", p=P), h2r[:]).then_inc(h2_out, 16)

            def route(b):
                pool.wait_ge(slot_ok, b + 1)
                if b == 0:
                    pool.wait_ge(pad_out, 48)
                for t in range(QT):
                    for c in range(2):
                        nc.gpsimd.indirect_dma_start(
                            out=info_d, out_offset=bass.IndirectOffsetOnAxis(ap=slot[:, t, c:c + 1], axis=0),
                            in_=info[:, t, c, :], in_offset=None).then_inc(routed, 16)

            for b in range(B - 1):
                rsqrt(1, b)
                keep_h2(b)
                if b == 0:
                    stack(3)
                route(b)

            def apart():
                pool.sem_inc(pool_waited, 1)

            def gather(i, par, src, rows=h2_d):
                j = 2 * i + par
                blk = pool.value_load(tblock_i[0:1, bass.ds(j, 1)], min_val=0, max_val=NB - 1)
                if not isinstance(i, int) or i:
                    pool.wait_ge(x_ps, j - 1)
                    apart()
                nc.gpsimd.tensor_copy(tokg[par][:], src[:, bass.ds(blk, 1), TOK]).then_inc(tokg_ok, 1)
                pool.wait_ge(tokg_ok, j + 1)
                apart()
                nc.gpsimd.indirect_dma_start(
                    out=xg[par][:], out_offset=None, in_=rows,
                    in_offset=bass.IndirectOffsetOnAxis(ap=tokg[par][:], axis=0)).then_inc(xg_in[par], 16)

            def add_rows(i, par, src):
                j = 2 * i + par
                blk = pool.value_load(tblock_i[0:1, bass.ds(j, 1)], min_val=0, max_val=NB - 1)
                if not isinstance(i, int) or i + par:
                    pool.wait_ge(y_added[1 - par], 16 * i + 16 * par)
                    apart()
                nc.gpsimd.tensor_copy(toka[par][:], src[:, bass.ds(blk, 1), TOK]).then_inc(toka_ok, 1)
                pool.wait_ge(toka_ok, j + 1)
                pool.wait_ge(ys_ok, j + 2)
                apart()
                nc.gpsimd.indirect_dma_start(
                    out=acc_d, out_offset=bass.IndirectOffsetOnAxis(ap=toka[par][:], axis=0),
                    in_=ys[par][:], in_offset=None, compute_op=ALU.add).then_inc(y_added[par], 16)

            def load_entries(n):
                pool.wait_ge(routed, 64 * (B - 1 + n))
                pool.dma_start(entries[n][:], info_d.rearrange("(p r) c -> p r c", p=P)).then_inc(entries_in, 16)

            def gather_j(j):
                if j == 0 or j == NA:
                    pool.wait_ge(plan_ok, 1 + j // NA)
                    pool.wait_ge(entries_in, 16 + 16 * (j // NA))
                if j < NA:
                    gather(j // 2, j % 2, entries[0], h2_d[0:(B - 1) * L])
                else:
                    gather(j // 2, j % 2, entries[1])

            def add_rows_j(j):
                add_rows(j // 2, j % 2, entries[j >= NA])

            pool.wait_ge(t_ps, NG * B)
            load_entries(0)
            pool.wait_ge(h2_out, 16 * (B - 1))
            gather_j(0)
            gather_j(1)
            rsqrt(1, B - 1)
            gather_j(2)
            keep_h2(B - 1)
            gather_j(3)
            route(B - 1)
            add_rows_j(0)
            gather_j(4)
            load_entries(1)
            add_rows_j(1)
            pool.wait_ge(h2_out, 16 * B)
            assert NA == 5
            for j in range(2, NA + 1):
                gather_j(j + 3)
                add_rows_j(j)
            n = (NT - 3) // 2
            with pool.Fori((NA + 1) // 2, n - 1) as i:
                for par in range(2):
                    gather(i + 1 + par, 1 - par, entries[1])
                    add_rows(i, par, entries[1])
            gather(n, 1, entries[1])
            add_rows(n - 1, 0, entries[1])
            gather(n + 1, 0, entries[1])
            for j in range(2 * n - 1, NT):
                add_rows_j(j)

            b = B - 2
            a = acc[:, QT * b:QT * b + QT, :]
            pool.wait_ge(acc_in[b], 16)
            link(nc.gpsimd.tensor_tensor(a, a, gates[:, GB, b, :].unsqueeze(1).broadcast_to([P, QT, D]), ALU.mult))
            pool.wait_ge(x2_ok, b + 1)
            nc.gpsimd.tensor_tensor(a, a, xs[:, QT * b:QT * b + QT, :], ALU.add).then_inc(pool_res_ok, 1)

        @block.scalar
        def _(act):
            act.wait_ge(c_in, 16)
            nc.scalar.activation(sc[:], cT_sb[:], ACT.Silu).then_inc(silu_ok, 1)

            def modulate(b):
                act.wait_ge(hT_ps, b + 1)
                act.wait_ge(modT_ok, 1)
                if b:
                    act.wait_ge(h_ok, b)
                for k in range(KC):
                    nc.scalar.activation(hT[:, k, :], ps_wk[:, k, :], ACT.Identity, scale=modT[:, 2 + k, b:b + 1],
                                         bias=modT[:, k, b:b + 1]).then_inc(hT_ok, 1)

            def keep_qk(b):
                act.wait_ge(small_in, 80)
                for i, (done, ready) in enumerate(((q_ps, qhi_ok), (k_ps, khi_ok))):
                    act.wait_ge(done, b + 1)
                    if b:
                        act.wait_ge(q_out[(b - 1) % 2], unloaded(b - 1))
                        act.wait_ge(k_out[(b - 1) % 2], unloaded(b - 1))
                    for m in range(KC):
                        last = nc.scalar.activation(qk[:, 2 * i, m, :], ps_qk[i][:, m, :], ACT.Identity,
                                                    bias=bqk[:, i, m:m + 1])
                    last.then_inc(ready, 1)

            def maxima(b):
                act.wait_ge(mT_ps, b + 1)
                if b:
                    act.wait_ge(m_in[(b - 1) % 2], landed(b - 1))
                nc.scalar.activation(mneg[:, 0, :], ps_w[0:HEADS, 0:L], ACT.Copy, scale=-1.0).then_inc(mhi_ok, 1)

            def exponentials(b, g):
                u = NG * b + g
                act.wait_ge(t_ps, u + 1)
                if u >= 4:
                    act.wait_ge(pv_ps, u // 2 - 1)
                nc.scalar.activation(probs[:, g % 4], ps_t[g % 2][:], ACT.Exp, scale=1.0 / DH).then_inc(exp_ok, 1)

            def keep_o(b, half):
                act.wait_ge(pv_ps, 4 * b + 2 * half + 2)
                if b:
                    act.wait_ge(tr1_ps, QT * b)
                nc.scalar.activation(oT[:, 2 * half:2 * half + 2, :], ps_pv[:], ACT.Copy).then_inc(oT_ok, 1)

            def split_o(b):
                act.wait_ge(tr2_ps, b + 1)
                if b:
                    act.wait_ge(wo_ps, b)
                nc.scalar.activation(ohi[:], ps_wk, ACT.Copy).then_inc(ohi_ok, 1)

            def keep_h2T(b):
                act.wait_ge(h2T_ps, b + 1)
                if b:
                    act.wait_ge(lg_ps, b)
                else:
                    act.wait_ge(pad_out, 48)
                nc.scalar.activation(h2T[:], ps_wk, ACT.Copy).then_inc(h2T_ok, 1)

            def exp_gap(b):
                act.wait_ge(dlt_ok, b + 1)
                nc.scalar.activation(edlt[:], dlt[:], ACT.Exp).then_inc(edlt_ok, 1)

            act.wait_ge(wraw_in[0], 48)
            nc.scalar.activation(whi[:, 0:3], w_raw[:, 0:3], ACT.Copy).then_inc(whi_ok, 1)
            modulate(0)
            keep_qk(0)
            modulate(1)
            act.wait_ge(mod_ps, 2)
            for n in (1, 2):
                nc.scalar.activation(mrow[32 * n:32 * n + B, :], ps_s[0][32 * n:32 * n + B].rearrange("p a b -> p (a b)"),
                                     ACT.Copy).then_inc(mrow23_ok, 1)
            act.wait_ge(wraw_in[1], 16)
            nc.scalar.activation(whi[:, 3], w_raw[:, 3], ACT.Copy).then_inc(whi_ok, 1)
            keep_qk(1)
            modulate(2)
            keep_qk(2)
            maxima(0)
            for b in range(B):
                if b == 1:
                    keep_qk(3)
                for g in range(NG):
                    exponentials(b, g)
                    if b:
                        if g == 2 - (b == B - 1):
                            split_o(b - 1)
                        elif g == 5 + (b == B - 1):
                            keep_h2T(b - 1)
                        elif g == 7:
                            if b + 1 < B:
                                maxima(b + 1)
                            exp_gap(b - 1)
                    if g == 5:
                        keep_o(b, 0)
                    if g == 6 and b == 0:
                        modulate(3)
                if b == 0:
                    maxima(1)
                keep_o(b, 1)

            def keep_x(i, par):
                j = 2 * i + par
                act.wait_ge(x_ps, j + 1)
                nc.scalar.activation(xhi[par][:], ps_x, ACT.Copy).then_inc(xhi_ok, 1)

            def expert(i, par):
                return act.value_load(texp_i[0:1, bass.ds(2 * i + par, 1)], min_val=0, max_val=NE - 1)

            def split_e(i, par, e):
                j = 2 * i + par
                if not isinstance(i, int) or i:
                    act.wait_ge(hid_ps, j - 1)
                for k in range(KC):
                    nc.scalar.activation(ehi[par][:, k, :], w01[:, bass.ds(e, 1), k, :], ACT.Copy).then_inc(ehi_ok, 1)

            def silu(i, par):
                j = 2 * i + par
                act.wait_ge(hid_ps, j + 1)
                act.wait_ge(inter_ok, j + 1)
                nc.scalar.activation(act0[par][:], ps_h[par][:, 0, :], ACT.Silu).then_inc(act0_ok, 1)

            def scale_y(i, par, src):
                j = 2 * i + par
                blk = act.value_load(tblock_i[0:1, bass.ds(j, 1)], min_val=0, max_val=NB - 1)
                act.wait_ge(y_ps, j + 1)
                if not isinstance(i, int) or i:
                    act.wait_ge(y_added[par], 16 * i)
                nc.scalar.activation(ys[par][:], ps_y, ACT.Copy,
                                     scale=src[:, bass.ds(blk, 1), WGT].bitcast(F32)).then_inc(ys_ok, 1)

            def split_ahead(j):
                i, par = (j + 3) // 2, (j + 3) % 2
                if j + 3 == NA:
                    act.wait_ge(plan_ok, 2)
                split_e(i, par, expert(i, par))

            def scale(j):
                if j == NA:
                    act.wait_ge(entries_in, 32)
                scale_y(j // 2, j % 2, entries[j >= NA])

            act.sem_inc(ys_ok, 1)
            act.wait_ge(plan_ok, 1)
            act.wait_ge(w01_in, 16 * 2 * NE)
            e = [expert(0, 0), expert(0, 1), expert(1, 0)]
            split_o(B - 1)
            split_e(0, 0, e[0])
            split_e(0, 1, e[1])
            act.wait_ge(entries_in, 16)
            keep_x(0, 0)
            keep_x(0, 1)
            silu(0, 0)
            split_e(1, 0, e[2])
            silu(0, 1)
            keep_h2T(B - 1)
            keep_x(1, 0)
            split_ahead(0)
            exp_gap(B - 1)
            scale(0)
            for j in range(1, NA + 1):
                silu((j + 1) // 2, (j + 1) % 2)
                keep_x((j + 2) // 2, j % 2)
                split_ahead(j)
                scale(j)
            n = (NT - 3) // 2
            with act.Fori((NA + 1) // 2, n) as i:
                e = [expert(i + 1, 1), expert(i + 2, 0)]
                for par in range(2):
                    silu(i + par, 1 - par)
                    keep_x(i + 1, par)
                    split_e(i + 1 + par, 1 - par, e[par])
                    scale_y(i, par, entries[1])
            silu(n, 1)
            keep_x(n + 1, 0)
            scale_y(n, 0, entries[1])
            silu(n + 1, 0)
            scale_y(n, 1, entries[1])
            scale_y(n + 1, 0, entries[1])

        @block.vector
        def _(dve):
            chain = [0]

            def link(ins):
                chain[0] += 1
                ins.then_inc(dve_chain, 1)
                dve.wait_ge(dve_chain, chain[0])

            def variance(ln, b):
                for t in range(QT):
                    link(nc.vector.bn_stats(stats[:, t, :], xs[:, QT * b + t, :]))
                    link(nc.vector.bn_aggr(mv[:, ln, QT * b + t, :], stats[:, t, :]))
                nc.vector.tensor_scalar(veps[:, ln, QT * b:QT * b + QT], mv[:, ln, QT * b:QT * b + QT, 1],
                                        EPS, None, ALU.add).then_inc(var_ok, 1)

            def normalise(b):
                dve.wait_ge(rstd_ok, b + 1)
                if b:
                    dve.wait_ge(hT_ps, b)
                for t in range(QT):
                    i = QT * b + t
                    last = nc.vector.tensor_scalar(h1n[:, t, :], xs[:, i, :], mv[:, 0, i, 0:1], rstd[:, 0, i:i + 1],
                                                   ALU.subtract, ALU.mult)
                last.then_inc(h1n_ok, 1)

            def split_h(b):
                dve.wait_ge(hT_ok, KC * (b + 1))
                if b:
                    dve.wait_ge(v_ps, b)
                link(nc.vector.tensor_copy(hhi[:], hT[:]))
                nc.vector.tensor_tensor(hlo[:], hT[:], hhi[:].bitcast(F32), ALU.subtract).then_inc(h_ok, 1)

            def keep_lo(b, i):
                dve.wait_ge((qhi_ok, khi_ok)[i], b + 1)
                for m in range(KC):
                    last = nc.vector.scalar_tensor_tensor(
                        out=qk[:, 2 * i + 1, m, :], in0=ps_qk[i][:, m, :], scalar=bqk[:, i, m:m + 1],
                        in1=qk[:, 2 * i, m, :].bitcast(F32), op0=ALU.add, op1=ALU.subtract)
                last.then_inc((qlo_ok, klo_ok)[i], 1)

            def keep_v(b):
                dve.wait_ge(v_ps, b + 1)
                if b == 0:
                    dve.wait_ge(ones_ok, 1)
                if b >= 3:
                    dve.wait_ge(pv_ps, 4 * (b - 2))
                for t in range(QT):
                    last = nc.vector.tensor_tensor(
                        va[:, b % 3, t, :, 0:DH], ps_v[:, t, :].rearrange("p (h d) -> p h d", h=HEADS),
                        bv_b[:].rearrange("p (h d) -> p h d", h=HEADS), ALU.add)
                last.then_inc(va_ok, 1)

            def keep_qkv(b):
                keep_lo(b, 0)
                keep_lo(b, 1)
                keep_v(b)

            def row_max(b, u):
                hp, qt, gg = u % 2, u // 8, u // 2 % 4
                dve.wait_ge(s_ps, 16 * b + u + 1)
                nc.vector.reduce_max(mx[:, b % 2, qt, NG * hp + 2 * gg:NG * hp + 2 * gg + 2], ps_s[hp][:],
                                     AX.X).then_inc(mx_ok, 1)

            def maxima(b):
                dve.wait_ge(mhi_ok, b + 1)
                nc.vector.scalar_tensor_tensor(out=mneg[:, 1, :], in0=ps_w[0:HEADS, 0:L], scalar=-1.0,
                                               in1=mneg[:, 0, :].bitcast(F32), op0=ALU.mult,
                                               op1=ALU.subtract).then_inc(mlo_ok, 1)

            def divide(b, qt):
                o = ps_w[:].rearrange("p (h c) -> p h c", h=HEADS)
                dve.wait_ge(tr1_ps, QT * b + qt + 1)
                link(nc.vector.reciprocal(rden[:], o[:, :, DH]))
                nc.vector.tensor_tensor(on[:, qt, :].rearrange("p (h d) -> p h d", h=HEADS), o[:, :, 0:DH],
                                        rden[:].unsqueeze(2).broadcast_to([P, HEADS, DH]),
                                        ALU.mult).then_inc(on_ok, 1)

            def split_o(b):
                dve.wait_ge(ohi_ok, b + 1)
                nc.vector.tensor_tensor(olo[:], ps_wk, ohi[:].bitcast(F32), ALU.subtract).then_inc(olo_ok, 1)

            def residual(b):
                dve.wait_ge(wo_ps, b + 1)
                dve.wait_ge(xb_ok, b + 1)
                ga = gates[:, GA, b, :].unsqueeze(1).broadcast_to([P, QT, D])
                link(nc.vector.tensor_tensor(on[:], ps_wk, ga, ALU.mult))
                s = xs[:, QT * b:QT * b + QT, :]
                nc.vector.tensor_tensor(s, on[:], s, ALU.add).then_inc(x2_ok, 1)

            def normalise2(b):
                dve.wait_ge(gates_in, 64)
                dve.wait_ge(rstd_ok, B + b + 1)
                if b:
                    dve.wait_ge(h2_out, 16 * b)
                    dve.wait_ge(h2T_ps, b)
                for t in range(QT):
                    i = QT * b + t
                    last = nc.vector.scalar_tensor_tensor(out=h2r[:, t, :], in0=xs[:, i, :], scalar=mv[:, 1, i, 0:1],
                                                          in1=gates[:, CB1, b, :], op0=ALU.subtract, op1=ALU.mult)
                link(last)
                for t in range(QT):
                    i = QT * b + t
                    last = nc.vector.scalar_tensor_tensor(out=h2r[:, t, :], in0=h2r[:, t, :], scalar=rstd[:, 1, i:i + 1],
                                                          in1=gates[:, SBI, b, :], op0=ALU.mult, op1=ALU.add)
                last.then_inc(h2_ok, 1)

            def choose(b):
                dve.wait_ge(lg_ps, b + 1)
                last = nc.vector.tensor_copy(lg[:], ps_w[:, 0:QT * NE].rearrange("p (t e) -> p t e", t=QT))
                last.then_inc(lg_ok, 1)
                dve.wait_ge(lg_ok, b + 1)
                for t in range(QT):
                    link(nc.vector.max(m8[:, t, :], lg[:, t, :]))
                    link(nc.vector.max_index(i8[:, t, :], m8[:, t, :], lg[:, t, :]))
                nc.vector.tensor_tensor(dlt[:], m8[:, :, 1], m8[:, :, 0], ALU.subtract).then_inc(dlt_ok, 1)
                link(nc.vector.tensor_copy(e12[:], i8[:, :, 0:2]))
                for t in range(QT):
                    last = nc.vector.tensor_tensor(hot[:, t], iota8[:].unsqueeze(1).broadcast_to([P, 2, NE]),
                                                   e12[:, t, :].unsqueeze(2).broadcast_to([P, 2, NE]), ALU.is_equal)
                    link(last)
                nc.vector.tensor_tensor(picked[:, QT * b:QT * b + QT, :], hot[:, :, 0, :], hot[:, :, 1, :],
                                        ALU.add).then_inc(picked_ok, 1)

            def weigh(b):
                dve.wait_ge(edlt_ok, b + 1)
                if b:
                    dve.wait_ge(routed, 64 * b)
                nc.vector.tensor_copy(info[:, :, :, TOK], token[:, QT * b:QT * b + QT].unsqueeze(2).broadcast_to([P, QT, 2]))
                link(nc.vector.tensor_scalar(wsum[:], edlt[:], 1.0, None, ALU.add))
                w = info[:, :, :, WGT].bitcast(F32)
                link(nc.vector.reciprocal(w[:, :, 0], wsum[:]))
                link(nc.vector.tensor_tensor(w[:, :, 1], edlt[:], w[:, :, 0], ALU.mult))

            def place(b):
                dve.wait_ge(rank_ps, b + 1)
                nc.vector.tensor_tensor(pos[:], ps_w[:, 0:QT * NE].rearrange("p (t e) -> p t e", t=QT),
                                        region[:].unsqueeze(1).broadcast_to([P, QT, NE]), ALU.add).then_inc(pos_ok, 1)
                dve.wait_ge(pos_ok, b + 1)
                for t in range(QT):
                    link(nc.vector.tensor_tensor(hot[:, t], hot[:, t], pos[:, t, :].unsqueeze(1).broadcast_to([P, 2, NE]),
                                                 ALU.mult))
                link(nc.vector.tensor_reduce(slotf[:], hot[:], AX.X, ALU.add))
                link(nc.vector.tensor_copy(slot_n[:], slotf[:]))
                link(nc.vector.tensor_scalar(slot_b[:], slot_n[:], 7, None, ALU.logical_shift_right))
                link(nc.vector.tensor_scalar(slot_p[:], slot_n[:], P - 1, None, ALU.bitwise_and))
                nc.vector.scalar_tensor_tensor(out=slot[:], in0=slot_p[:], scalar=float(NB), in1=slot_b[:],
                                               op0=ALU.mult, op1=ALU.add).then_inc(slot_ok, 1)

            def keep_count(n, up):
                dve.wait_ge(count_ps, n + 1)
                nc.vector.tensor_scalar(count[:], ps_w[:, 0:NE], up, None, ALU.add).then_inc(count_ok, 1)
                dve.wait_ge(count_ok, n + 1)
                link(nc.vector.tensor_scalar(count[:], count[:], 7, None, ALU.logical_shift_right))
                link(nc.vector.tensor_copy(tiles[:], count[:]))

            def plan(n):
                if n:
                    link(nc.vector.tensor_tensor(tiles[:], tiles[:], taken[:], ALU.subtract))
                link(nc.vector.tensor_tensor_scan(tend[:], ones8[:], tiles[:], 0.0, ALU.mult, ALU.add))
                link(nc.vector.tensor_tensor(tbeg[:], tend[:], tiles[:], ALU.subtract))
                link(nc.vector.tensor_scalar(pick[:], tend[:], part_no[:], None, ALU.is_le))
                link(nc.vector.tensor_reduce(texp[:], pick[:], AX.X, ALU.add))
                link(nc.vector.tensor_scalar(pick[:], iota8[:], texp[:], None, ALU.is_equal))
                if n:
                    link(nc.vector.tensor_tensor(tbeg[:], tbeg[:], taken[:], ALU.subtract))
                link(nc.vector.tensor_tensor(pick[:], pick[:], tbeg[:], ALU.mult))
                link(nc.vector.tensor_reduce(tbase[:], pick[:], AX.X, ALU.add))
                link(nc.vector.tensor_tensor(tblock[:], part_no[:], tbase[:], ALU.subtract))
                link(nc.vector.scalar_tensor_tensor(out=tblock[:], in0=texp[:], scalar=float(T), in1=tblock[:],
                                                    op0=ALU.mult, op1=ALU.add))
                nc.vector.tensor_scalar(tblock[:], tblock[:], NB - 1.0, None, ALU.min)
                nc.vector.tensor_scalar(texp[:], texp[:], NE - 1.0, None, ALU.min).then_inc(plan_col, 1)

            def keep_taken():
                link(nc.vector.tensor_scalar(taken[:], tbeg[:], -1.0, float(NA), ALU.mult, ALU.add))
                link(nc.vector.tensor_tensor(taken[:], taken[:], tiles[:], ALU.min))
                link(nc.vector.tensor_scalar(taken[:], taken[:], 0.0, None, ALU.max))

            def keep_plan(n):
                dve.wait_ge(plan_ps, n + 1)
                dve.wait_ge(t_ps, NG * B)
                rows = ps_plan[n]
                j = slice(0, NA) if n == 0 else slice(NA, NT)
                nc.vector.tensor_copy(tblock_i[:, j], rows[0:1, 0:j.stop - j.start])
                nc.vector.tensor_copy(texp_i[:, j], rows[0:1, P:P + j.stop - j.start]).then_inc(plan_ok, 1)

            def split_weights(i, s):
                dve.wait_ge(whi_ok, i + 1)
                nc.vector.tensor_tensor(wlo[:, s], w_raw[:, s], whi[:, s].bitcast(F32),
                                        ALU.subtract).then_inc(wsplit_ok, 1)

            dve.wait_ge(x_in[0], 16)
            variance(0, 0)
            normalise(0)
            split_weights(0, slice(0, 3))
            dve.wait_ge(mod_ps, 1)
            nc.vector.tensor_copy(mrow[0:B, :], ps_s[0][0:B].rearrange("p a b -> p (a b)")).then_inc(mrow_ok, 1)
            dve.wait_ge(modT_ps, 1)
            nc.vector.tensor_copy(modT[:, 0:2, :], ps_s[1][:, 0, 0:2 * B].rearrange("p (j b) -> p j b", j=2))
            nc.vector.tensor_scalar(modT[:, 2:4, :], ps_s[1][:, 0, 2 * B:4 * B].rearrange("p (j b) -> p j b", j=2),
                                    1.0, None, ALU.add).then_inc(modT_ok, 1)
            split_h(0)
            dve.wait_ge(x_in[1], 16)
            variance(0, 1)
            normalise(1)
            keep_qkv(0)
            split_h(1)
            split_weights(1, slice(3, 4))
            dve.wait_ge(x_in[2], 16)
            variance(0, 2)
            dve.wait_ge(x_in[3], 16)
            variance(0, 3)
            keep_qkv(1)
            def guard(r, c):
                g, s, a = mrow[r:r + B, c:c + D], gsign[r:r + B, :], gabs[r:r + B, :]
                link(nc.vector.tensor_scalar(s, g, 0.0, 2.0, ALU.is_ge, ALU.mult))
                link(nc.vector.scalar_tensor_tensor(out=a, in0=s, scalar=-1.0, in1=g, op0=ALU.add, op1=ALU.mult))
                link(nc.vector.tensor_scalar(a, a, 0.25, None, ALU.max))
                nc.vector.scalar_tensor_tensor(out=g, in0=s, scalar=-1.0, in1=a, op0=ALU.add,
                                               op1=ALU.mult).then_inc(gate_rows, 1)

            dve.wait_ge(mrow23_ok, 2)
            cb = mrow[64:64 + B, 0:D]
            nc.vector.tensor_scalar(cb, cb, 1.0, None, ALU.add)
            normalise(2)
            for u in range(16):
                row_max(0, u)
                if u == 3:
                    split_h(2)
                elif u in (9, 13):
                    keep_lo(2, u // 12)
            maxima(0)
            keep_v(2)
            for b in range(B):
                if b == 1:
                    keep_qkv(3)
                for u in range(16):
                    if b + 1 < B:
                        row_max(b + 1, u)
                    if b == 0:
                        if u == 3:
                            guard(32, 0)
                            guard(64, D)
                        elif u == 9:
                            normalise(3)
                        elif u == 15:
                            maxima(1)
                            split_h(3)
                    elif u in (3, 5):
                        divide(b - 1, u // 4)
                    elif u == 7:
                        split_o(b - 1)
                    elif u == 9:
                        residual(b - 1)
                        dve.wait_ge(x2_ok, b)
                        variance(1, b - 1)
                    elif u == 11:
                        normalise2(b - 1)
                    elif u == 15:
                        choose(b - 1)
                        if b + 1 < B:
                            maxima(b + 1)
                        weigh(b - 1)
                        place(b - 1)
            def gate_up(i, par):
                j = 2 * i + par
                dve.wait_ge(act0_ok, j + 1)
                nc.vector.tensor_tensor(inter[par][:], ps_h[par][:, 1, :], act0[par][:], ALU.mult).then_inc(inter_ok, 1)

            def keep_i(i, par):
                j = 2 * i + par
                dve.wait_ge(i_ps, j + 1)
                nc.vector.tensor_copy(iT[par][:].rearrange("p m t -> p (m t)"), ps_i).then_inc(iT_ok, 1)

            def split_x(i, par):
                j = 2 * i + par
                dve.wait_ge(xhi_ok, j + 1)
                nc.vector.tensor_tensor(xlo[par][:], ps_x, xhi[par][:].bitcast(F32), ALU.subtract).then_inc(xlo_ok, 1)

            def expert(i, par):
                return dve.value_load(texp_i[0:1, bass.ds(2 * i + par, 1)], min_val=0, max_val=NE - 1)

            def split_e(i, par, e, chunks=range(KC)):
                j = 2 * i + par
                for k in chunks:
                    dve.wait_ge(ehi_ok, KC * j + k + 1)
                    nc.vector.tensor_tensor(elo[par][:, k, :], w01[:, bass.ds(e, 1), k, :].rearrange("p e f -> p (e f)"),
                                            ehi[par][:, k, :].bitcast(F32), ALU.subtract).then_inc(elo_ok, 1)

            dve.sem_inc(inter_ok, 2)
            dve.sem_inc(iT_ok, 1)
            keep_count(0, 0.0)
            plan(0)
            divide(B - 1, 0)
            keep_plan(0)
            dve.wait_ge(plan_ok, 1)
            divide(B - 1, 1)
            split_o(B - 1)
            keep_taken()
            split_e(0, 0, expert(0, 0))
            residual(B - 1)
            split_x(0, 0)
            dve.wait_ge(x2_ok, B)
            variance(1, B - 1)
            split_e(0, 1, expert(0, 1))
            split_x(0, 1)
            e = [expert(1, 0), expert(1, 1)]
            normalise2(B - 1)
            gate_up(0, 0)
            gate_up(0, 1)
            keep_i(0, 0)
            split_x(1, 0)
            split_e(1, 0, e[0], [0])
            choose(B - 1)
            split_e(1, 0, e[0], range(1, KC))
            weigh(B - 1)
            place(B - 1)
            keep_i(0, 1)
            split_e(1, 1, e[1])
            keep_count(1, P - 1.0)
            gate_up(1, 0)
            split_x(1, 1)
            plan(1)
            keep_i(1, 0)
            keep_plan(1)
            split_e(2, 0, expert(2, 0))
            dve.wait_ge(plan_ok, 2)
            n = (NT - 3) // 2
            with dve.Fori(1, n) as i:
                e = [expert(i + 1, 1), expert(i + 2, 0)]
                for par in range(2):
                    gate_up(i + par, 1 - par)
                    split_x(i + 1, par)
                    split_e(i + 1 + par, 1 - par, e[par], [0])
                    keep_i(i + par, 1 - par)
                    split_e(i + 1 + par, 1 - par, e[par], range(1, KC))
            gate_up(n, 1)
            split_x(n + 1, 0)
            keep_i(n, 1)
            gate_up(n + 1, 0)
            keep_i(n + 1, 0)

            for b in (*range(B - 2), B - 1):
                a = acc[:, QT * b:QT * b + QT, :]
                dve.wait_ge(acc_in[b], 16)
                link(nc.vector.tensor_tensor(a, a, gates[:, GB, b, :].unsqueeze(1).broadcast_to([P, QT, D]), ALU.mult))
                nc.vector.tensor_tensor(a, a, xs[:, QT * b:QT * b + QT, :], ALU.add).then_inc(res_ok, 1)

        @block.tensor
        def _(pe):
            w_reader = [None]

            def take_w():
                if w_reader[0]:
                    pe.wait_ge(*w_reader[0])

            def three(out, stat, mov, first, last):
                for i, (s, m) in enumerate(((stat[0], mov[0]), (stat[0], mov[1]), (stat[1], mov[0]))):
                    ins = nc.tensor.matmul(out, s, m, start=first and i == 0, stop=last and i == 2)
                return ins

            def h_columns(b):
                pe.wait_ge(h1n_ok, b + 1)
                take_w()
                for k in range(KC):
                    for t in range(QT):
                        last = nc.tensor.transpose(ps_wk[:, k, P * t:P * t + P], h1n[:, t, P * k:P * k + P], ident[:])
                last.then_inc(hT_ps, 1)
                w_reader[0] = (hT_ok, KC * (b + 1))

            def project_part(b, n):
                if n == 0:
                    pe.wait_ge(wsplit_ok, 1)
                    pe.wait_ge(h_ok, b + 1)
                    if b >= 3:
                        pe.wait_ge(exp_ok, NG * (b - 2))
                    elif b >= 1:
                        pe.wait_ge(klo_ok, b)
                if n == 4 and b in (1, 2):
                    pe.wait_ge(va_ok, b)
                i, m = n // 2, n % 2
                c = slice(P * m, P * m + P)
                for k in range(KC):
                    if i < 2:
                        last = three(ps_qk[i][:, m, :], (whi[:, i, k, c], wlo[:, i, k, c]),
                                     (hhi[:, k, :], hlo[:, k, :]), k == 0, k == KC - 1)
                    else:
                        last = three(ps_v[:, m, :], (hhi[:, k, c], hlo[:, k, c]),
                                     (whi[:, 2, k, :], wlo[:, 2, k, :]), k == 0, k == KC - 1)
                if m == 1:
                    last.then_inc((q_ps, k_ps, v_ps)[i], 1)

            def project(b):
                for n in range(6):
                    project_part(b, n)

            def score(b, u):
                p, hp, qt, gg = b % 2, u % 2, u // 8, u // 2 % 4
                if u == 0:
                    pe.wait_ge(stack_in[p], 2 * landed(b))
                    pe.wait_ge(third_in[p], landed(b))
                if 16 * b + u >= 2:
                    pe.wait_ge(mx_ok, 16 * b + u - 1)
                r = HR * hp
                for i in range(2):
                    g = 2 * gg + i
                    last = nc.tensor.matmul(ps_s[hp][:, i, :], qs[r:r + K_MAX, p, g, P * qt:P * qt + P],
                                            ks[r:r + K_MAX, p, g, :], start=True, stop=True)
                last.then_inc(s_ps, 1)

            def maxima(b):
                pe.wait_ge(mx_ok, 16 * (b + 1))
                take_w()
                for qt in range(QT):
                    last = nc.tensor.transpose(ps_w[0:HEADS, P * qt:P * qt + P], mx[:, b % 2, qt, :], ident[:])
                last.then_inc(mT_ps, 1)
                w_reader[0] = (mlo_ok, b + 1)

            def score_T(b, g):
                p, u = b % 2, NG * b + g
                if g == 0:
                    pe.wait_ge(m_in[p], landed(b))
                    done = min(b + 3, B)
                    pe.wait_ge(klo_ok, done)
                    pe.wait_ge(va_ok, done)
                if u >= 2:
                    pe.wait_ge(exp_ok, u - 1)
                for hp in range(2):
                    r = HR * hp
                    for kc in range(QT):
                        last = nc.tensor.matmul(ps_t[g % 2][:, hp, L * kc:L * kc + L],
                                                ks[r:r + K_SUB, p, g, P * kc:P * kc + P],
                                                qs[r:r + K_SUB, p, g, :], start=True, stop=True)
                last.then_inc(t_ps, 1)

            def weighted(b, n):
                pe.wait_ge(exp_ok, NG * b + 2 * n + 2)
                if n % 2 == 0 and 4 * b + n:
                    pe.wait_ge(oT_ok, 2 * b + n // 2)
                for kc in range(QT):
                    for h in range(4 * n, 4 * n + 4):
                        r = 32 * (h % 4)
                        last = nc.tensor.matmul(ps_pv[r:r + 32, n % 2, :], va[:, b % 3, kc, h, :],
                                                probs[:, h // 2 % 4, h % 2, L * kc:L * kc + L],
                                                start=kc == 0, stop=kc == QT - 1)
                last.then_inc(pv_ps, 1)

            def o_rows(b, qt):
                pe.wait_ge(oT_ok, 2 * (b + 1))
                take_w()
                for n in range(HEADS // 4):
                    last = nc.tensor.transpose(ps_w[:, P * n:P * n + P], oT[:, n, P * qt:P * qt + P], ident[:])
                last.then_inc(tr1_ps, 1)
                w_reader[0] = (on_ok, QT * b + qt + 1)

            def o_columns(b):
                pe.wait_ge(on_ok, QT * (b + 1))
                take_w()
                for k in range(KC):
                    for qt in range(QT):
                        last = nc.tensor.transpose(ps_wk[:, k, P * qt:P * qt + P], on[:, qt, P * k:P * k + P], ident[:])
                last.then_inc(tr2_ps, 1)
                w_reader[0] = (olo_ok, b + 1)

            def project_o(b):
                pe.wait_ge(olo_ok, b + 1)
                take_w()
                pe.wait_ge(wsplit_ok, 2)
                for qt in range(QT):
                    for k in range(KC):
                        c = slice(P * qt, P * qt + P)
                        last = three(ps_wk[:, qt, :], (ohi[:, k, c], olo[:, k, c]),
                                     (whi[:, 3, k, :], wlo[:, 3, k, :]), k == 0, k == KC - 1)
                last.then_inc(wo_ps, 1)
                w_reader[0] = (x2_ok, b + 1)

            def h2_columns(b):
                pe.wait_ge(h2_ok, b + 1)
                take_w()
                for k in range(KC):
                    for t in range(QT):
                        last = nc.tensor.transpose(ps_wk[:, k, P * t:P * t + P], h2r[:, t, P * k:P * k + P], ident[:])
                last.then_inc(h2T_ps, 1)
                w_reader[0] = (h2T_ok, b + 1)

            def logits(b):
                take_w()
                for t in range(QT):
                    for k in range(KC):
                        last = nc.tensor.matmul(ps_w[:, NE * t:NE * t + NE], h2T[:, k, P * t:P * t + P],
                                                gate_sb[:, k, :], start=k == 0, stop=k == KC - 1)
                last.then_inc(lg_ps, 1)
                w_reader[0] = (lg_ok, b + 1)

            def counts(batches):
                take_w()
                for n in range(QT * batches):
                    last = nc.tensor.matmul(ps_w[:, 0:NE], ones_bf[:], picked[:, n, :],
                                            start=n == 0, stop=n == QT * batches - 1)
                last.then_inc(count_ps, 1)
                w_reader[0] = (count_ok, 1 if batches < B else 2)

            def plan_rows(n):
                pe.wait_ge(plan_col, n + 1)
                if n:
                    take_w()
                nc.tensor.transpose(ps_plan[n][0:1, 0:P], tblock[:], ident[:])
                nc.tensor.transpose(ps_plan[n][0:1, P:2 * P], texp[:], ident[:]).then_inc(plan_ps, 1)

            def ranks(b):
                pe.wait_ge(picked_ok, b + 1)
                pe.wait_ge(const_ok, 1)
                take_w()
                for t in range(QT):
                    i = QT * b + t
                    for n in range(i + 1):
                        last = nc.tensor.matmul(ps_w[:, NE * t:NE * t + NE], upper[:] if n == i else ones_bf[:],
                                                picked[:, n, :], start=n == 0, stop=n == i)
                last.then_inc(rank_ps, 1)
                w_reader[0] = (pos_ok, b + 1)

            pe.wait_ge(ident_ok, 1)
            h_columns(0)

            def modulation(thirds):
                for k in range(KC):
                    for n in thirds:
                        last = nc.tensor.matmul(ps_s[0][32 * n:32 * n + B].rearrange("p a b -> p (a b)"), sc[:, k, :],
                                                wmod_sb[:, k, 2 * D * n:2 * D * n + 2 * D],
                                                start=k == 0, stop=k == KC - 1)
                last.then_inc(mod_ps, 1)

            pe.wait_ge(silu_ok, 1)
            pe.wait_ge(wmod_in[0], 16)
            modulation((0,))
            pe.wait_ge(mrow_ok, 1)
            for j in range(4):
                last = nc.tensor.transpose(ps_s[1][:, 0, B * j:B * j + B], mrow[0:B, P * j:P * j + P], ident[0:B, 0:B])
            last.then_inc(modT_ps, 1)
            project(0)
            h_columns(1)
            pe.wait_ge(wmod_in[1], 32)
            modulation((1, 2))
            project(1)
            pe.wait_ge(mrow23_ok, 2)
            for u in range(16):
                score(0, u)
                if u == 1:
                    h_columns(2)
                elif u in range(3, 15, 2):
                    project_part(2, (u - 3) // 2)
            maxima(0)
            for b in range(B):
                late = b == B - 1
                if b == 1:
                    project(3)
                for g in range(NG):
                    if 0 < g < NG - 1:
                        score_T(b, g)
                    if b + 1 < B and g < NG - 1:
                        for u in range(4) if g == 0 else (2 * g + 2, 2 * g + 3):
                            score(b + 1, u)
                    if g == NG - 2:
                        score_T(b, NG - 1)
                    if g in (2, 4, 6):
                        weighted(b, g // 2 - 1)
                    if b:
                        if late and g == 0:
                            o_rows(b - 1, 0)
                            o_rows(b - 1, 1)
                        elif g < QT and not late:
                            o_rows(b - 1, g)
                        elif g == 2 - late:
                            o_columns(b - 1)
                        elif g == 3 - late:
                            project_o(b - 1)
                        elif g == 5 + late:
                            h2_columns(b - 1)
                        elif g == 6 + late:
                            logits(b - 1)
                    if g == 0:
                        score_T(b, g)
                    if g == 6 and b == 0:
                        h_columns(3)
                if b + 1 < B:
                    maxima(b + 1)
                weighted(b, 3)
                if b and b + 1 < B:
                    ranks(b - 1)
            ranks(B - 2)
            def columns_x(i, par):
                j = 2 * i + par
                pe.wait_ge(xg_in[par], 16 * i + 16)
                if not isinstance(j, int) or j:
                    pe.wait_ge(xlo_ok, j)
                for k in range(KC):
                    last = nc.tensor.transpose(ps_x[:, k, :], xg[par][:, P * k:P * k + P], ident[:])
                last.then_inc(x_ps, 1)

            def expert(i, par):
                return pe.value_load(texp_i[0:1, bass.ds(2 * i + par, 1)], min_val=0, max_val=NE - 1)

            def hidden(i, par, halves=(0, 1)):
                j = 2 * i + par
                if 0 in halves:
                    pe.wait_ge(xlo_ok, j + 1)
                    pe.wait_ge(inter_ok, j + 1)
                    pe.wait_ge(elo_ok, KC * j + KC)
                for n in halves:
                    for k in range(KC):
                        f = slice(F * n, F * n + F)
                        last = three(ps_h[par][:, n, :], (xhi[par][:, k, :], xlo[par][:, k, :]),
                                     (ehi[par][:, k, f], elo[par][:, k, f]), k == 0, k == KC - 1)
                if 1 in halves:
                    last.then_inc(hid_ps, 1)

            def columns_i(i, par):
                j = 2 * i + par
                pe.wait_ge(inter_ok, j + 3)
                pe.wait_ge(iT_ok, j + 1)
                for m in range(FC):
                    last = nc.tensor.transpose(ps_i[:, P * m:P * m + P], inter[par][:, P * m:P * m + P], ident[:])
                last.then_inc(i_ps, 1)

            def down(i, par, e):
                j = 2 * i + par
                pe.wait_ge(iT_ok, j + 2)
                pe.wait_ge(ys_ok, j + 1)
                for m in range(FC):
                    last = nc.tensor.matmul(ps_y, iT[par][:, m, :], wex[:, bass.ds(e, 1), m, :],
                                            start=m == 0, stop=m == FC - 1)
                last.then_inc(y_ps, 1)

            counts(B - 1)
            o_rows(B - 1, 0)
            plan_rows(0)
            o_rows(B - 1, 1)
            o_columns(B - 1)
            project_o(B - 1)
            pe.wait_ge(plan_ok, 1)
            pe.wait_ge(oT_ok, 2 * B)
            pe.wait_ge(exp_ok, NG * B)
            columns_x(0, 0)
            e = expert(0, 0)
            columns_x(0, 1)
            hidden(0, 0)
            hidden(0, 1)
            h2_columns(B - 1)
            columns_i(0, 0)
            columns_x(1, 0)
            logits(B - 1)
            pe.wait_ge(wex_in, 16 * NE)
            down(0, 0, e)
            ranks(B - 1)
            for j in range(1, NA + 1):
                if j == NA - 1:
                    pe.wait_ge(plan_ok, 2)
                e = expert(j // 2, j % 2)
                columns_i(j // 2, j % 2)
                hidden((j + 1) // 2, (j + 1) % 2)
                if j == 1:
                    counts(B)
                if j == 2:
                    plan_rows(1)
                columns_x((j + 2) // 2, j % 2)
                down(j // 2, j % 2, e)
            n = (NT - 3) // 2
            with pe.Fori((NA + 1) // 2, n) as i:
                e = [expert(i, 0), expert(i, 1)]
                for par in range(2):
                    columns_i(i, par)
                    hidden(i + par, 1 - par)
                    columns_x(i + 1, par)
                    down(i, par, e[par])
            e = [expert(n, 0), expert(n, 1), expert(n + 1, 0)]
            columns_i(n, 0)
            hidden(n, 1)
            columns_x(n + 1, 0)
            down(n, 0, e[0])
            columns_i(n, 1)
            hidden(n + 1, 0)
            down(n, 1, e[1])
            columns_i(n + 1, 0)
            down(n + 1, 0, e[2])


def kernel(**inputs):
    import numpy as np
    import concourse.bacc as bacc
    from concourse.bass_utils import run_bass_kernel_spmd

    nc = bacc.Bacc("TRN2", target_bir_lowering=False, num_devices=1)
    given = {n: np.asarray(a) for n, a in inputs.items()}
    names = ["L0_attn_x", "L0_attn_Wq", "L0_attn_bq", "L0_attn_Wk", "L0_attn_bk", "L0_attn_Wv", "L0_attn_bv",
             "L0_attn_Wo", "L0_attn_bo", "L0_ffn_gate_kernel", "L0_ffn_w0_kernel", "L0_ffn_w1_kernel",
             "L0_ffn_wo_kernel", "L0_c", "L0_wmod"]
    given["L0_c"] = given["L0_c"].T
    for n in ("L0_attn_bq", "L0_attn_bk"):
        given[n] = given[n].reshape(KC, P).T
    arrays, args = {}, []
    for n in names:
        a = np.ascontiguousarray(given[n])
        arrays[n] = a
        args.append(nc.dram_tensor(n, a.shape, mybir.dt.from_np(a.dtype), kind="ExternalInput").ap())
    out = nc.dram_tensor("out", (B, L, D), F32, kind="ExternalOutput").ap()
    adaln_block(nc, *args, out)
    r = run_bass_kernel_spmd(nc, [arrays], core_ids=[0])
    return r.results[0]["out"]
```
